# Optimizing a Trainium2 kernel written in Bass

```python
import numpy as np
import jax
import jax.numpy as jnp

def _softmax(x, axis=-1):
    return jax.nn.softmax(x, axis=axis)

def _gelu(x):
    return jax.nn.gelu(x, approximate=True)

def _silu(x):
    return jax.nn.silu(x)

def _sigmoid(x):
    return jax.nn.sigmoid(x)

def _layernorm(x, axis=-1, eps=1e-05):
    m = jnp.mean(x, axis=axis, keepdims=True)
    v = jnp.var(x, axis=axis, keepdims=True)
    return (x - m) / jnp.sqrt(v + eps)

def _scatter_add(tgt, idx, src, axis=0):
    return tgt.at[idx].add(src)

def _segment_sum(src, seg, n):
    return jax.ops.segment_sum(src, seg, n)
kernel_name = 'mk_gnn_preln_d2_gnn_r64_35de19'

def setup_inputs(seed: int=0):
    np.random.seed(seed)
    _w = jnp.asarray

    def _rec_inputs():
        import jax
        import jax.numpy as jnp
        _gk = jax.random.key(seed)
        x = -0.0003713 + 1 * jax.random.normal(jax.random.fold_in(_gk, 1), (50000, 128), jnp.float32)
        src = jax.random.randint(jax.random.fold_in(_gk, 2), (25000,), 0, 50000, jnp.int32)
        dst = jnp.minimum((50000 * jax.random.uniform(jax.random.fold_in(_gk, 3), (25000,)) ** 2.0).astype(jnp.int32), 49999)
        _o = jnp.argsort(dst, stable=True)
        src = src[_o]
        dst = dst[_o]
        edge_attr_128 = 5.93493e-05 + 1.00006 * jax.random.normal(jax.random.fold_in(_gk, 11), (25000, 128), jnp.float32)
        return (x, src, dst, edge_attr_128)
    x, src, dst, edge_attr_128 = _rec_inputs()

    def _L0_gnn_setup():
        import jax, jax.numpy as jnp
        import numpy as np
        N_NODES = 100000
        N_EDGES = 25000
        D_IN = 128
        D_OUT = 128
        key = jax.random.key(seed)
        k1, k2, k3, k4 = jax.random.split(key, 4)
        node_feature = jax.random.normal(k1, (N_NODES, D_IN), dtype=jnp.float32)
        scale = 1.0 / np.sqrt(D_IN)
        W_l = jax.random.normal(k2, (D_OUT, D_IN), dtype=jnp.float32) * scale
        W_r = jax.random.normal(k3, (D_OUT, D_IN), dtype=jnp.float32) * scale
        edge_index = jax.random.randint(k4, (2, N_EDGES), 0, N_NODES, dtype=jnp.int64)
        return {'node_feature': node_feature, 'W_l': W_l, 'W_r': W_r, 'edge_index': edge_index}
    _L0_gnn_all = _L0_gnn_setup()
    _L0_gnn_in = {k: v for k, v in _L0_gnn_all.items() if k in ('W_l', 'W_r')}
    del _L0_gnn_all

    def _L1_gnn_setup():
        import jax, jax.numpy as jnp
        import numpy as np
        N_NODES = 50000
        N_EDGES = 9375
        D = 128
        BN_EPS = 1e-05

        def _linear_init(key, fan_in, fan_out):
            kw, kb = jax.random.split(key)
            bound = 1.0 / np.sqrt(fan_in)
            W = jax.random.uniform(kw, (fan_in, fan_out), minval=-bound, maxval=bound, dtype=jnp.float32)
            b = jax.random.uniform(kb, (fan_out,), minval=-bound, maxval=bound, dtype=jnp.float32)
            return (W, b)

        def _bn(h, gamma, beta):
            mean = jnp.mean(h, axis=0)
            var = jnp.var(h, axis=0)
            return (h - mean) * jax.lax.rsqrt(var + BN_EPS) * gamma + beta
        key = jax.random.key(seed)
        ks = jax.random.split(key, 8)
        x = jax.random.normal(ks[0], (N_NODES, D), dtype=jnp.float32)
        edge_index = jax.random.randint(ks[1], (2, N_EDGES), 0, N_NODES, dtype=jnp.int32)
        edge_attr = jax.random.normal(ks[2], (N_EDGES, D), dtype=jnp.float32)
        W1, b1 = _linear_init(ks[3], 2 * D, D)
        W2, b2 = _linear_init(ks[4], D, D)
        W3, b3 = _linear_init(ks[5], D, D)
        g1 = jnp.ones((D,), jnp.float32)
        be1 = jnp.zeros((D,), jnp.float32)
        g2 = jnp.ones((D,), jnp.float32)
        be2 = jnp.zeros((D,), jnp.float32)
        return {'x': x, 'edge_index': edge_index, 'edge_attr': edge_attr, 'W1': W1, 'b1': b1, 'g1': g1, 'be1': be1, 'W2': W2, 'b2': b2, 'g2': g2, 'be2': be2, 'W3': W3, 'b3': b3}
    _L1_gnn_all = _L1_gnn_setup()
    _L1_gnn_in = {k: v for k, v in _L1_gnn_all.items() if k in ('W1', 'b1', 'g1', 'be1', 'W2', 'b2', 'g2', 'be2', 'W3', 'b3')}
    del _L1_gnn_all
    return {'x': x, 'src': src, 'dst': dst, 'edge_attr_128': edge_attr_128, 'L0_gnn_W_l': _L0_gnn_in['W_l'], 'L0_gnn_W_r': _L0_gnn_in['W_r'], 'L1_gnn_W1': _L1_gnn_in['W1'], 'L1_gnn_b1': _L1_gnn_in['b1'], 'L1_gnn_g1': _L1_gnn_in['g1'], 'L1_gnn_be1': _L1_gnn_in['be1'], 'L1_gnn_W2': _L1_gnn_in['W2'], 'L1_gnn_b2': _L1_gnn_in['b2'], 'L1_gnn_g2': _L1_gnn_in['g2'], 'L1_gnn_be2': _L1_gnn_in['be2'], 'L1_gnn_W3': _L1_gnn_in['W3'], 'L1_gnn_b3': _L1_gnn_in['b3']}

def reference(x, src, dst, edge_attr_128, L0_gnn_W_l, L0_gnn_W_r, L1_gnn_W1, L1_gnn_b1, L1_gnn_g1, L1_gnn_be1, L1_gnn_W2, L1_gnn_b2, L1_gnn_g2, L1_gnn_be2, L1_gnn_W3, L1_gnn_b3):
    import jax
    import jax.numpy as jnp

    def _L0_gnn_ref(node_feature, W_l, W_r, edge_index):
        import jax, jax.numpy as jnp
        import numpy as np
        N_NODES = 100000
        N_EDGES = 25000
        D_IN = 128
        D_OUT = 128
        'PyG SAGEConv (mean aggr, root_weight=True, bias=False):\n               out_i = W_l @ mean_{j in N(i)} x_j + W_r @ x_i\n            Messages flow edge_index[0] (src) -> edge_index[1] (dst).'
        src = edge_index[0]
        dst = edge_index[1]
        n = node_feature.shape[0]
        msg = node_feature[src]
        summed = jax.ops.segment_sum(msg, dst, num_segments=n)
        deg = jax.ops.segment_sum(jnp.ones((src.shape[0],), dtype=node_feature.dtype), dst, num_segments=n)
        agg = summed / jnp.maximum(deg, 1.0)[:, None]
        return agg @ W_l.T + node_feature @ W_r.T

    def _L1_gnn_ref(x, edge_index, edge_attr, W1, b1, g1, be1, W2, b2, g2, be2, W3, b3):
        import jax, jax.numpy as jnp
        import numpy as np
        N_NODES = 50000
        N_EDGES = 9375
        D = 128
        BN_EPS = 1e-05

        def _linear_init(key, fan_in, fan_out):
            kw, kb = jax.random.split(key)
            bound = 1.0 / np.sqrt(fan_in)
            W = jax.random.uniform(kw, (fan_in, fan_out), minval=-bound, maxval=bound, dtype=jnp.float32)
            b = jax.random.uniform(kb, (fan_out,), minval=-bound, maxval=bound, dtype=jnp.float32)
            return (W, b)

        def _bn(h, gamma, beta):
            mean = jnp.mean(h, axis=0)
            var = jnp.var(h, axis=0)
            return (h - mean) * jax.lax.rsqrt(var + BN_EPS) * gamma + beta
        src = edge_index[0]
        agg = jax.ops.segment_sum(edge_attr, src, num_segments=x.shape[0])
        h = jnp.concatenate([x, agg], axis=1)
        h = _bn(jax.nn.silu(h @ W1 + b1), g1, be1)
        h = _bn(jax.nn.silu(h @ W2 + b2), g2, be2)
        return h @ W3 + b3
    edge_index = jnp.stack([src, dst])
    h = jnp.maximum(_layernorm(x, axis=-1), 0.0)
    x = x + _L0_gnn_ref(h, L0_gnn_W_l, L0_gnn_W_r, edge_index)
    h = jnp.maximum(_layernorm(x, axis=-1), 0.0)
    x = x + _L1_gnn_ref(h, edge_index, edge_attr_128, L1_gnn_W1, L1_gnn_b1, L1_gnn_g1, L1_gnn_be1, L1_gnn_W2, L1_gnn_b2, L1_gnn_g2, L1_gnn_be2, L1_gnn_W3, L1_gnn_b3)
    return x

_drawn_inputs = setup_inputs


def setup_inputs(seed=0):
    import zlib

    import numpy as np

    out = dict(_drawn_inputs(seed))
    spreads = {'L1_gnn_g1': (1.0, 0.2),
     'L1_gnn_be1': (0.0, 0.8),
     'L1_gnn_g2': (1.0, 0.2),
     'L1_gnn_be2': (0.0, 0.1)}
    factors = {'L1_gnn_b1': 8.0, 'L1_gnn_b2': 7.475}
    for name, (base, spread) in spreads.items():
        noise = np.random.default_rng([zlib.crc32(name.encode()), seed]).standard_normal(out[name].shape)
        drawn = base * np.exp(spread * noise) if base else spread * noise
        out[name] = jnp.asarray(drawn.astype(out[name].dtype))
    for name, factor in factors.items():
        out[name] = (out[name] * factor).astype(out[name].dtype)
    return out
```

```python
from contextlib import ExitStack

import concourse.bass as bass
from concourse import mybir

P = 128
ROWS = 4
GROUP = P * ROWS
CHUNKS = 2 * ROWS
ROUND = 2 * GROUP


def this(sem, par, i, inc=1):
    return sem[par], (i + 1) * inc


def two_ago(sem, par, i, inc=1):
    return sem[par], i * inc


def last(sem, par, i, inc=1):
    return sem[1 - par], (i + par) * inc


def gnn_layers(nc, x, src, dst, edge_attr, WlT, WrT, W1, b1, g1, be1, W2, b2, g2, be2, W3, b3, out):
    fp32 = mybir.dt.float32
    fp16 = mybir.dt.float16
    i32 = mybir.dt.int32
    u32 = mybir.dt.uint32
    ALU = mybir.AluOpType
    ACT = mybir.ActivationFunctionType

    N, D = x.shape
    E = src.shape[0]
    EPS = 1e-5

    RF = N // ROUND
    IT = RF // 2
    NODE_TAIL = [P, (N - RF * ROUND - GROUP) // ROWS]
    EDGE_TAIL = (E - RF * GROUP) // ROWS
    assert RF % 2 == 0 and E // GROUP == RF and GROUP + NODE_TAIL[1] * ROWS == N - RF * ROUND
    assert EDGE_TAIL * ROWS == E - RF * GROUP and 0 < EDGE_TAIL <= P and 0 < NODE_TAIL[1] <= P
    KEPT = min(15, IT)
    ACC_ROWS = P * -(-(N + 2 * P) // P)
    ZCOLS = ACC_ROWS * D // P // 12
    assert ZCOLS * 12 * P == ACC_ROWS * D
    ZHALF = ZCOLS * 12 // IT
    assert ZHALF * IT == ZCOLS * 12
    COLS = (RF + 1) * CHUNKS

    def node_rows(t):
        full = t[0:RF * ROUND, :].rearrange("(r n p j) d -> r p n (j d)", n=2, p=P, j=ROWS)
        a = t[RF * ROUND:RF * ROUND + GROUP, :].rearrange("(p j) d -> p (j d)", j=ROWS)
        b = t[RF * ROUND + GROUP:N, :].rearrange("(p j) d -> p (j d)", j=ROWS)
        return full, (a, b)

    def edge_cols(t):
        return (t[0:RF * GROUP].rearrange("(r p j) -> r p j", p=P, j=ROWS),
                t[RF * GROUP:E].rearrange("(p j) -> p j", j=ROWS))

    acc1 = nc.dram_tensor("acc1", (ACC_ROWS, D), fp32).ap()
    acc2 = nc.dram_tensor("acc2", (ACC_ROWS, D), fp32).ap()
    y_dram = nc.dram_tensor("y_dram", (N, D), fp32).ap()
    x1_dram = nc.dram_tensor("x1_dram", (N, D), fp32).ap()
    z_dram = nc.dram_tensor("z_dram", (RF - 2 * KEPT + 2, P, ROUND), fp32).ap()
    zz_dram = nc.dram_tensor("zz_dram", (RF - 2 * KEPT + 2, P, ROUND), fp32).ap()
    zy_dram = nc.dram_tensor("zy_dram", (RF - 2 * KEPT + 2, P, ROUND), fp32).ap()

    x_v, y_v, x1_v, out_v = (node_rows(t) for t in (x, y_dram, x1_dram, out))
    acc1_v, acc2_v = node_rows(acc1[0:N, :]), node_rows(acc2[0:N, :])
    src_v, dst_v = edge_cols(src), edge_cols(dst)
    src_row = src[0:RF * GROUP].rearrange("(r k) -> r k", k=GROUP)
    dst_row = dst[0:RF * GROUP].rearrange("(r k) -> r k", k=GROUP)
    ea_v = (edge_attr[0:RF * GROUP, :].rearrange("(r p j) d -> r p (j d)", p=P, j=ROWS),
            edge_attr[RF * GROUP:E, :].rearrange("(p j) d -> p (j d)", j=ROWS))
    acc1_z = acc1.rearrange("(p r) d -> p (r d)", p=P).rearrange("p (k c) -> k p c", k=12)
    acc2_z = acc2.rearrange("(p r) d -> p (r d)", p=P).rearrange("p (k c) -> k p c", k=IT)

    def column(t):
        return t.rearrange("(p a) -> p a", a=1)

    ctx = ExitStack()
    with ctx:
        def sb(name, shape, dt=fp32):
            return ctx.enter_context(nc.sbuf_tensor(name, shape, dt))

        def sem(name):
            return ctx.enter_context(nc.semaphore(name))

        def pair(name):
            return [sem(f"{name}_{k}") for k in range(2)]

        wl = sb("wl", [P, D]); wr = sb("wr", [P, D]); w1a = sb("w1a", [P, D]); w1b = sb("w1b", [P, D])
        w2 = sb("w2", [P, D]); w3 = sb("w3", [P, D]); w2s = sb("w2s", [P, D])
        b3b = sb("b3b", [P, D])
        vecs = sb("vecs", [P, 6])
        ident = sb("ident", [P, P])
        order = sb("order", [P, 2, P])
        eps = sb("eps", [P, 1])
        iota_p = sb("iota_p", [P, P], fp16)
        iota_c = sb("iota_c", [P, COLS], fp16)
        warm = sb("warm", [P, 1])
        rd = sb("rd", [P, 2, CHUNKS])
        dump = sb("dump", [P, 2])
        raw = sb("raw", [P, 2, (RF + 1) * ROWS], i32)
        ints = sb("ints", [P, 2, (RF + 1) * ROWS], i32)
        dst_tab = sb("dst_tab", [P, RF + 1, 4, ROWS])
        src_tab = sb("src_tab", [P, RF + 1, 2, ROWS])
        rdeg = sb("rdeg", [P, COLS])
        xin = sb("xin", [P, 2, CHUNKS, D])
        aux = sb("aux", [P, 2, CHUNKS, D])
        res = sb("res", [P, 2, CHUNKS, D])
        hT = sb("hT", [P, 2, CHUNKS, P])
        rows = sb("rows", [P, 2, ROWS, D])
        hE = sb("hE", [P, 2, ROWS, D])
        same = sb("same", [P, 2, 2, 3, P])
        sumT = sb("sumT", [P, 2, ROWS, P])
        vrow = sb("vrow", [P, 2, ROWS, D])
        irow = sb("irow", [P, 2, GROUP], i32)
        icol = sb("icol", [P, 2, ROWS], u32)
        cols = sb("cols", [P, 2, 4, ROWS])
        count = sb("count", [P, 2, ROWS])
        shift = sb("shift", [P, 2, ROWS])
        target = sb("target", [P, 2, ROWS], u32)
        hotp = sb("hotp", [P, ROWS, P], fp16)
        hotc = sb("hotc", [P, ROWS, COLS], fp16)
        st6 = sb("st6", [P, 2, 12, 6])
        mv = sb("mv", [P, 2, 12, 2])
        sd = sb("sd", [P, 2, 12])
        rs = sb("rs", [P, 2, 12])
        nm = sb("nm", [P, 2, ROWS])
        bst = sb("bst", [P, 2 * (RF + 1), 6])
        bn = sb("bn", [P, 2, 8])
        zT = sb("zT", [P, 2 * KEPT, ROUND])
        zs = hT
        zeros = zT[:, :, :].rearrange("p r c -> p (r c)")[:, 0:max(ZCOLS, ZHALF)]

        ps = ctx.enter_context(nc.psum_tensor("ps", [P, 8, 512], fp32))
        psR = ps[:, 0:2, :].rearrange("p b (j c) -> p (b j) c", c=P)
        psQ = ps[:, 2:4, :].rearrange("p b (j c) -> p (b j) c", c=P)
        psA = ps[:, 4, :].rearrange("p (j c) -> p j c", c=P)
        psV = ps[:, 5, :].rearrange("p (j c) -> p j c", c=P)
        psH = ps[:, 6, 0:COLS]
        psB = ps[:, 7, :]
        ps2 = [ps[:, 2 * k:2 * k + 2, :].rearrange("p b (j c) -> p (b j) c", c=P) for k in range(2)]

        s_w = sem("weights_loaded")
        s_idx = sem("indices_loaded")
        s_const = sem("constants_made")
        s_mem = sem("memsets_done")
        s_chain = sem("vector_chain")
        s_tab = sem("tables_made")
        s_zero1 = sem("acc1_zeroed")
        s_zero2 = sem("acc2_zeroed")
        s_turn = sem("pool_turn")
        s_eps = sem("eps_set")

        def phase(tag, names):
            return {k: pair(f"{tag}_{k}") for k in names.split()}

        common = ("x_loaded row_loaded rows_loaded mv_ready sd_ready rs_ready normed nm_ready targets transposed "
                  "relu product summed sum_copied v_ready v_copied added stored")
        A = phase("a", common + " icol_loaded h_ready hot_ready hot_used cols_read")
        B = phase("b", common + " a_loaded z_copied z_stored")
        C = phase("c", "loaded z_loaded transposed added silu stats stored")
        F = phase("f", "z_loaded product silu stats stored")
        G = phase("g", "x_loaded z_loaded scaled product biased done stored")
        s_sc1 = pair("acc1_scattered")
        s_sc2 = pair("acc2_scattered")
        s_z0 = sem("hist_opened")
        s_zeros = sem("zeros_made")
        s_bn = pair("bn_steps")
        s_bw = sem("bn_bias_product")

        block = ctx.enter_context(nc.Block())

        def pieces(tail):
            return [(slice(0, ROWS), NODE_TAIL[0]), (slice(ROWS, CHUNKS), NODE_TAIL[1])] if tail else \
                [(slice(0, CHUNKS), P)]

        def chunk_parts(tail):
            return [(c, NODE_TAIL[c // ROWS] if tail else P) for c in range(CHUNKS)]

        def edge_parts(tail):
            return EDGE_TAIL if tail else P

        def flat(t, par, c, p):
            return t[0:p, par, c, :].rearrange("p c d -> p (c d)")

        def rounds(eng, body, lo=0, hi=IT):
            if hi > lo:
                for par in range(2):
                    body(lo, par, False)
            if hi > lo + 1:
                with eng.Fori(lo + 1, hi) as i:
                    for par in range(2):
                        body(i, par, False)

        @block.sync
        def _(sp):
            for t, w in ((wl, WlT), (wr, WrT), (w1a, W1[0:D, :]), (w1b, W1[D:2 * D, :]), (w2, W2), (w3, W3)):
                sp.dma_start(t[:, :], w).then_inc(s_w, 16)
            for k, v in enumerate((b1, g1, be1, b2, g2, be2)):
                sp.dma_start(vecs[:, k:k + 1], column(v)).then_inc(s_w, 16)
            sp.dma_start(b3b[:, :], b3.partition_broadcast(P)).then_inc(s_w, 16)
            sp.wait_ge(s_mem, 1)
            for k, v in enumerate((dst_v, src_v)):
                sp.dma_start(raw[:, k, 0:RF * ROWS].rearrange("p (r j) -> p r j", j=ROWS),
                             v[0].rearrange("r p j -> p r j")).then_inc(s_idx, 16)
                sp.dma_start(raw[0:EDGE_TAIL, k, RF * ROWS:], v[1]).then_inc(s_idx, 16)

            def load_nodes(t, v, par, r, tail, sems):
                if tail:
                    for n in range(2):
                        p = NODE_TAIL[n]
                        sp.dma_start(t[0:p, par, n * ROWS:(n + 1) * ROWS, :].rearrange("p j d -> p (j d)"),
                                     v[1][n]).then_inc(sems[par], 16)
                else:
                    sp.dma_start(t[:, par, :, :].rearrange("p (n j) d -> p n (j d)", n=2),
                                 v[0][r]).then_inc(sems[par], 16)

            def store_nodes(t, v, par, r, tail, sems):
                if tail:
                    for n in range(2):
                        p = NODE_TAIL[n]
                        sp.dma_start(v[1][n], t[0:p, par, n * ROWS:(n + 1) * ROWS, :]
                                     .rearrange("p j d -> p (j d)")).then_inc(sems[par], 16)
                else:
                    sp.dma_start(v[0][r], t[:, par, :, :].rearrange("p (n j) d -> p n (j d)", n=2))\
                        .then_inc(sems[par], 16)

            def load_a(i, par, tail):
                r = 2 * i + par
                sp.wait_ge(*two_ago(A["added"], par, i))
                load_nodes(xin, x_v, par, r, tail, A["x_loaded"])
                sp.wait_ge(*two_ago(A["rows_loaded"], par, i, 64))
                sp.wait_ge(*two_ago(A["targets"], par, i))
                if tail:
                    sp.dma_start(icol[0:EDGE_TAIL, par, :], src_v[1].bitcast(u32)).then_inc(A["icol_loaded"][par], 16)
                    sp.dma_start(irow[:, par, 0:EDGE_TAIL * ROWS],
                                 dst[RF * GROUP:E].partition_broadcast(P)).then_inc(A["row_loaded"][par], 16)
                else:
                    sp.dma_start(icol[:, par, :], src_v[0][r].bitcast(u32)).then_inc(A["icol_loaded"][par], 16)
                    sp.dma_start(irow[:, par, :], dst_row[r].partition_broadcast(P)).then_inc(A["row_loaded"][par], 16)

            def store_a(i, par, tail):
                sp.wait_ge(*this(A["added"], par, i))
                store_nodes(res, y_v, par, 2 * i + par, tail, A["stored"])

            load_a(0, 0, False)
            load_a(0, 1, False)
            sp.wait_ge(s_zeros, 1)
            for k in range(12):
                sp.dma_start(acc1_z[k], zeros[:, 0:ZCOLS]).then_inc(s_zero1, 16)
            with sp.Fori(0, IT - 1) as i:
                sp.dma_start(acc2_z[i], zeros[:, 0:ZHALF]).then_inc(s_zero2, 16)
                for par in range(2):
                    store_a(i, par, False)
                    load_a(i + 1, par, False)
            sp.dma_start(acc2_z[IT - 1], zeros[:, 0:ZHALF]).then_inc(s_zero2, 16)
            store_a(IT - 1, 0, False)
            load_a(IT, 0, True)
            store_a(IT - 1, 1, False)
            store_a(IT, 0, True)

            def load_b(i, par, tail):
                r = 2 * i + par
                sp.wait_ge(*two_ago(B["added"], par, i))
                load_nodes(xin, y_v, par, r, tail, B["x_loaded"])
                sp.wait_ge(*two_ago(B["transposed"], par, i))
                load_nodes(aux, acc1_v, par, r, tail, B["a_loaded"])
                sp.wait_ge(*two_ago(B["summed"], par, i))
                if tail:
                    sp.dma_start(rows[0:EDGE_TAIL, par, :, :].rearrange("p j d -> p (j d)"), ea_v[1])\
                        .then_inc(B["rows_loaded"][par], 16)
                else:
                    sp.dma_start(rows[:, par, :, :].rearrange("p j d -> p (j d)"), ea_v[0][r])\
                        .then_inc(B["rows_loaded"][par], 16)
                sp.wait_ge(*two_ago(B["targets"], par, i))
                if tail:
                    sp.dma_start(irow[:, par, 0:EDGE_TAIL * ROWS],
                                 src[RF * GROUP:E].partition_broadcast(P)).then_inc(B["row_loaded"][par], 16)
                else:
                    sp.dma_start(irow[:, par, :], src_row[r].partition_broadcast(P)).then_inc(B["row_loaded"][par], 16)

            def store_b(i, par, tail, spill):
                sp.wait_ge(*this(B["added"], par, i))
                store_nodes(res, x1_v, par, 2 * i + par, tail, B["stored"])
                if spill:
                    sp.wait_ge(*this(B["z_copied"], par, i))
                    spill_store(z_dram, i, par, tail, B["z_stored"])

            def spill_store(d, i, par, tail, sems):
                r = 2 * i + par - 2 * KEPT
                if tail:
                    for c, p in ((slice(0, ROWS), NODE_TAIL[0]), (slice(ROWS, CHUNKS), NODE_TAIL[1])):
                        sp.dma_start(d[r].rearrange("f (c q) -> f c q", q=P)[:, c, 0:p], zs[:, par, c, 0:p])\
                            .then_inc(sems[par], 16)
                else:
                    sp.dma_start(d[r], zs[:, par, :, :].rearrange("p c q -> p (c q)")).then_inc(sems[par], 16)

            def spill_load(d, i, par, tail, sems):
                r = 2 * i + par - 2 * KEPT
                if tail:
                    for c, p in ((slice(0, ROWS), NODE_TAIL[0]), (slice(ROWS, CHUNKS), NODE_TAIL[1])):
                        sp.dma_start(zs[:, par, c, 0:p], d[r].rearrange("f (c q) -> f c q", q=P)[:, c, 0:p])\
                            .then_inc(sems[par], 16)
                else:
                    sp.dma_start(zs[:, par, :, :].rearrange("p c q -> p (c q)"), d[r]).then_inc(sems[par], 16)

            sp.wait_ge(*this(A["stored"], 1, IT - 1, 16))
            sp.wait_ge(A["stored"][0], 16 * (IT + 2))
            sp.wait_ge(*this(s_sc1, 0, IT, 64))
            sp.wait_ge(*this(s_sc1, 1, IT - 1, 64))
            sp.wait_ge(*this(A["transposed"], 0, IT))
            sp.wait_ge(*this(A["targets"], 0, IT))
            load_b(0, 0, False)
            load_b(0, 1, False)
            for lo, hi, spill in ((0, KEPT, False), (KEPT, IT - 1, True)):
                if hi > lo:
                    with sp.Fori(lo, hi) as i:
                        for par in range(2):
                            store_b(i, par, False, spill)
                            load_b(i + 1, par, False)
            spill = KEPT < IT
            store_b(IT - 1, 0, False, spill)
            load_b(IT, 0, True)
            store_b(IT - 1, 1, False, spill)
            store_b(IT, 0, True, True)

            def load_c(i, par, tail, spill):
                sp.wait_ge(*two_ago(C["transposed"], par, i))
                load_nodes(xin, acc2_v, par, 2 * i + par, tail, C["loaded"])
                if spill:
                    sp.wait_ge(C["stored"][par], (i - KEPT) * 16)
                    spill_load(z_dram, i, par, tail, C["z_loaded"])

            def stream(load, store):
                load(0, 0, False, KEPT == 0)
                load(0, 1, False, KEPT == 0)
                if KEPT - 1 > 0:
                    with sp.Fori(0, KEPT - 1) as i:
                        for par in range(2):
                            store(i, par, False, False)
                            load(i + 1, par, False, False)
                for i in range(KEPT - 1, KEPT):
                    for par in range(2):
                        store(i, par, False, False)
                        if i + 1 < IT:
                            load(i + 1, par, False, True)
                        elif par == 0:
                            load(i + 1, 0, True, True)
                if KEPT < IT:
                    with sp.Fori(KEPT, IT - 1) as i:
                        for par in range(2):
                            store(i, par, False, True)
                            load(i + 1, par, False, True)
                    store(IT - 1, 0, False, True)
                    load(IT, 0, True, True)
                    store(IT - 1, 1, False, True)
                store(IT, 0, True, True)

            sp.wait_ge(*this(s_sc2, 0, IT, 64))
            sp.wait_ge(*this(s_sc2, 1, IT - 1, 64))
            sp.wait_ge(*this(B["stored"], 1, IT - 1, 16))
            sp.wait_ge(B["stored"][0], 16 * (IT + 2))
            sp.wait_ge(B["z_stored"][0], 16 * (IT - KEPT + 2))
            if KEPT < IT:
                sp.wait_ge(B["z_stored"][1], 16 * (IT - KEPT))

            def store_c(i, par, tail, spill):
                if spill:
                    sp.wait_ge(*this(C["silu"], par, i))
                    sp.wait_ge(*this(C["stats"], par, i))
                    spill_store(zz_dram, i, par, tail, C["stored"])

            stream(load_c, store_c)

            def load_f(i, par, tail, spill):
                if spill:
                    sp.wait_ge(F["stored"][par], (i - KEPT) * 16)
                    spill_load(zz_dram, i, par, tail, F["z_loaded"])

            def store_f(i, par, tail, spill):
                if spill:
                    sp.wait_ge(*this(F["silu"], par, i))
                    sp.wait_ge(*this(F["stats"], par, i))
                    spill_store(zy_dram, i, par, tail, F["stored"])

            sp.wait_ge(C["stored"][0], 16 * (IT - KEPT + 2))
            if KEPT < IT:
                sp.wait_ge(C["stored"][1], 16 * (IT - KEPT))
            stream(load_f, store_f)

            def load_g(i, par, tail, spill):
                sp.wait_ge(*two_ago(G["done"], par, i))
                load_nodes(xin, x1_v, par, 2 * i + par, tail, G["x_loaded"])
                if spill:
                    sp.wait_ge(*two_ago(G["product"], par, i))
                    spill_load(zy_dram, i, par, tail, G["z_loaded"])

            def store_g(i, par, tail, spill):
                sp.wait_ge(*this(G["done"], par, i))
                store_nodes(res, out_v, par, 2 * i + par, tail, G["stored"])

            sp.wait_ge(F["stored"][0], 16 * (IT - KEPT + 2))
            if KEPT < IT:
                sp.wait_ge(F["stored"][1], 16 * (IT - KEPT))
            stream(load_g, store_g)
            sp.wait_ge(*this(G["stored"], 1, IT - 1, 16))
            sp.wait_ge(G["stored"][0], 16 * (IT + 2))

        @block.gpsimd
        def _(pool):
            nc.gpsimd.memset(raw[:, :, :], 0).then_inc(s_mem, 1)
            nc.gpsimd.memset(ident[:, :], 0.0).then_inc(s_turn, 1)
            nc.gpsimd.memset(order[:, :, :], 1.0).then_inc(s_turn, 1)
            pool.wait_ge(s_turn, 2)
            nc.gpsimd.affine_select(out=ident[:, :], in_=ident[:, :], compare_op=ALU.not_equal, fill=1.0,
                                    base=0, pattern=[[-1, P]], channel_multiplier=1).then_inc(s_const, 1)
            nc.gpsimd.affine_select(out=order[:, 1, :], in_=order[:, 1, :], compare_op=ALU.is_ge, fill=0.0,
                                    base=0, pattern=[[-1, P]], channel_multiplier=1).then_inc(s_const, 1)
            nc.gpsimd.iota(iota_p[:, :], [[1, P]], base=0, channel_multiplier=0,
                           allow_small_or_imprecise_dtypes=True).then_inc(s_const, 1)
            nc.gpsimd.iota(iota_c[:, :], [[1, COLS]], base=0, channel_multiplier=0,
                           allow_small_or_imprecise_dtypes=True).then_inc(s_const, 1)
            nc.gpsimd.iota(dump[:, :], [[P, 2]], base=N, channel_multiplier=1,
                           allow_small_or_imprecise_dtypes=True).then_inc(s_const, 1)

            def hold(s, value):
                pool.wait_ge(s, value)
                pool.sem_inc(s_turn, 1)

            def gather(i, par, tail):
                p = edge_parts(tail)
                hold(*this(A["icol_loaded"], par, i, 16))
                hold(*two_ago(A["h_ready"], par, i))
                for j in range(ROWS):
                    pool.indirect_dma_start(
                        rows[0:p, par, j, :], None, x,
                        bass.IndirectOffsetOnAxis(ap=icol[0:p, par, j:j + 1], axis=0))\
                        .then_inc(A["rows_loaded"][par], 16)

            def scatter(ph, acc, s_sc, i, par, tail):
                p = edge_parts(tail)
                hold(*this(ph["v_copied"], par, i))
                hold(*this(ph["targets"], par, i))
                for h in range(2):
                    if h:
                        hold(s_sc[par], i * 64 + 32)
                    else:
                        hold(*last(s_sc, par, i, 64))
                    for j in (2 * h, 2 * h + 1):
                        pool.indirect_dma_start(
                            acc, bass.IndirectOffsetOnAxis(ap=target[0:p, par, j:j + 1], axis=0),
                            vrow[0:p, par, j, :], None, compute_op=ALU.add).then_inc(s_sc[par], 16)

            gather(0, 0, False)
            gather(0, 1, False)
            pool.wait_ge(s_zero1, 16 * 12)
            for par in range(2):
                scatter(A, acc1, s_sc1, 0, par, False)
                gather(1, par, False)
            with pool.Fori(1, IT - 1) as i:
                for par in range(2):
                    scatter(A, acc1, s_sc1, i, par, False)
                    gather(i + 1, par, False)
            scatter(A, acc1, s_sc1, IT - 1, 0, False)
            gather(IT, 0, True)
            scatter(A, acc1, s_sc1, IT - 1, 1, False)
            scatter(A, acc1, s_sc1, IT, 0, True)
            pool.wait_ge(s_zero2, 16 * IT)
            rounds(pool, lambda i, par, tail: scatter(B, acc2, s_sc2, i, par, tail))
            scatter(B, acc2, s_sc2, IT, 0, True)

            def bias(i, par, tail):
                hold(*((G["x_loaded"][0], 16 * (IT + 2)) if tail else this(G["x_loaded"], par, i, 16)))
                for c, p in pieces(tail):
                    t = xin[0:p, par, c, :]
                    ins = nc.gpsimd.tensor_tensor(t, t, b3b[0:p, :].unsqueeze(1).broadcast_to(
                        [p, c.stop - c.start, D]), ALU.add)
                ins.then_inc(G["biased"][par], 1)

            pool.wait_ge(s_w, 16 * 13)
            rounds(pool, bias)
            bias(IT, 0, True)

        @block.scalar
        def _(act):
            act.wait_ge(s_eps, 1)
            nc.scalar.activation(warm[:, :], eps[:, :], ACT.Sqrt)

            def roots(ph, i, par, n):
                act.wait_ge(*this(ph["mv_ready"], par, i))
                nc.scalar.activation(sd[:, par, 0:n], mv[:, par, 0:n, 1], ACT.Sqrt, bias=eps[:, :])\
                    .then_inc(ph["sd_ready"][par], 1)

            def relu(ph, i, par, tail, free):
                act.wait_ge(*this(ph["transposed"], par, i))
                free(i, par)
                for c, p in pieces(tail):
                    ins = nc.scalar.activation(hT[:, par, c, 0:p], psR[:, c, 0:p], ACT.Relu)
                ins.then_inc(ph["relu"][par], 1)

            def sums(ph, s_sc, i, par, tail):
                p = edge_parts(tail)
                act.wait_ge(*this(ph["summed"], par, i))
                act.wait_ge(*two_ago(ph["v_ready"], par, i))
                nc.scalar.activation(sumT[:, par, :, 0:p], psA[:, :, 0:p], ACT.Copy).then_inc(ph["sum_copied"][par], 1)
                act.wait_ge(*this(ph["v_ready"], par, i))
                act.wait_ge(*two_ago(s_sc, par, i, 64))
                nc.scalar.activation(vrow[0:p, par, :, :], psV[0:p, :, :], ACT.Copy).then_inc(ph["v_copied"][par], 1)

            def round_a(i, par, tail):
                p = edge_parts(tail)
                roots(A, i, par, 12)
                relu(A, i, par, tail, lambda i, par: act.wait_ge(*two_ago(A["product"], par, i)))
                act.wait_ge(*this(A["nm_ready"], par, i))
                act.wait_ge(*two_ago(A["summed"], par, i))
                for j in range(ROWS):
                    ins = nc.scalar.activation(hE[0:p, par, j, :], rows[0:p, par, j, :], ACT.Relu,
                                               bias=nm[0:p, par, j:j + 1], scale=rs[0:p, par, j:j + 1])
                ins.then_inc(A["h_ready"][par], 1)
                sums(A, s_sc1, i, par, tail)

            rounds(act, round_a)
            round_a(IT, 0, True)

            def round_b(spill):
                def body(i, par, tail):
                    roots(B, i, par, 12)

                    def free(i, par):
                        act.wait_ge(*two_ago(B["product"], par, i))
                        if spill:
                            act.wait_ge(B["z_stored"][par], (i - KEPT) * 16)
                    relu(B, i, par, tail, free)
                    act.wait_ge(*this(B["product"], par, i))
                    for c, p in pieces(tail):
                        if spill:
                            dst_ap = zs[:, par, c, 0:p]
                        else:
                            dst_ap = zT[:, 2 * i + par, :].rearrange("p (c q) -> p c q", q=P)[:, c, 0:p]
                        ins = nc.scalar.activation(dst_ap, psQ[:, c, 0:p], ACT.Copy)
                    ins.then_inc(B["z_copied"][par], 1)
                    sums(B, s_sc2, i, par, tail)
                return body

            act.wait_ge(s_zero1, 16 * 12)
            act.wait_ge(s_zero2, 16 * IT)
            act.wait_ge(s_w, 16 * 13)
            rounds(act, round_b(False), 0, KEPT)
            rounds(act, round_b(True), KEPT, IT)
            round_b(True)(IT, 0, True)

            def z_of(i, par, c, p, spill):
                if spill:
                    return zs[:, par, c, 0:p]
                return zT[:, 2 * i + par, :].rearrange("p (c q) -> p c q", q=P)[:, c, 0:p]

            def silu_c(spill):
                def body(i, par, tail):
                    act.wait_ge(*this(C["added"], par, i))
                    for c, p in pieces(tail):
                        t = z_of(i, par, c, p, spill)
                        ins = nc.scalar.activation(t, t, ACT.Silu, bias=vecs[:, 0:1])
                    ins.then_inc(C["silu"][par], 1)
                return body

            nc.scalar.activation(warm[:, :], eps[:, :], ACT.Silu)
            rounds(act, silu_c(False), 0, KEPT)
            rounds(act, silu_c(True), KEPT, IT)
            silu_c(True)(IT, 0, True)

            def bn_root(k):
                act.wait_ge(s_bn[k], 1)
                nc.scalar.activation(bn[:, k, 2:3], bn[:, k, 1:2], ACT.Sqrt, bias=eps[:, :]).then_inc(s_bn[k], 1)

            bn_root(0)
            act.wait_ge(s_bn[0], 8)
            nc.scalar.activation(warm[:, :], eps[:, :], ACT.Silu)

            def silu_f(spill):
                def body(i, par, tail):
                    act.wait_ge(*this(F["product"], par, i))
                    for c, p in pieces(tail):
                        ins = nc.scalar.activation(z_of(i, par, c, p, spill), ps2[par][:, c, 0:p], ACT.Silu,
                                                   bias=bn[:, 0, 7:8])
                    ins.then_inc(F["silu"][par], 1)
                return body

            rounds(act, silu_f(False), 0, KEPT)
            rounds(act, silu_f(True), KEPT, IT)
            silu_f(True)(IT, 0, True)
            bn_root(1)
            act.wait_ge(s_bn[1], 6)
            act.wait_ge(F["stored"][0], 16 * (IT - KEPT + 2))
            if KEPT < IT:
                act.wait_ge(F["stored"][1], 16 * (IT - KEPT))

            def scale_g(spill):
                def body(i, par, tail):
                    if spill:
                        act.wait_ge(G["z_loaded"][par], (i - KEPT + 1) * 16 + (16 if tail else 0))
                    else:
                        act.wait_ge(*two_ago(G["product"], par, i))
                    for c, p in pieces(tail):
                        ins = nc.scalar.activation(hT[:, par, c, 0:p], z_of(i, par, c, p, spill), ACT.Identity,
                                                   bias=bn[:, 1, 6:7], scale=bn[:, 1, 4:5])
                    ins.then_inc(G["scaled"][par], 1)
                return body

            rounds(act, scale_g(False), 0, KEPT)
            rounds(act, scale_g(True), KEPT, IT)
            scale_g(True)(IT, 0, True)

        @block.vector
        def _(dve):
            done = [0]

            def link(ins):
                done[0] += 1
                ins.then_inc(s_chain, 1)
                dve.wait_ge(s_chain, done[0])

            nc.vector.memset(eps[:, :], EPS).then_inc(s_eps, 1)
            nc.vector.memset(hotc[:, :, :], 0.0).then_inc(s_z0, 1)
            nc.vector.memset(zeros, 0.0).then_inc(s_zeros, 1)
            link(nc.vector.memset(mv[:, :, :, :], 1.0))
            dve.wait_ge(s_z0, 2)
            dve.wait_ge(s_idx, 64)
            dve.wait_ge(s_const, 5)
            for k, tab in enumerate((dst_tab, src_tab)):
                r3 = raw[:, k, :].rearrange("p (r j) -> p r j", j=ROWS)
                link(nc.vector.tensor_copy(tab[:, :, 0, :], r3))
                for h in range(2):
                    nc.vector.tensor_scalar(tab[:, :, 1, h:ROWS:2], tab[:, :, 0, h:ROWS:2],
                                            -1.0, dump[:, h:h + 1], ALU.mult, ALU.add)
            link(nc.vector.tensor_scalar(ints[:, 0, :], raw[:, 0, :], 2, P - 1, ALU.logical_shift_right,
                                         ALU.bitwise_and))
            nc.vector.tensor_copy(dst_tab[:, :, 2, :], ints[:, 0, :].rearrange("p (r j) -> p r j", j=ROWS))
            link(nc.vector.tensor_scalar(ints[:, 1, :], raw[:, 0, :], 9, None, ALU.logical_shift_right))
            link(nc.vector.tensor_scalar(ints[:, 0, :], raw[:, 0, :], ROWS - 1, None, ALU.bitwise_and))
            link(nc.vector.scalar_tensor_tensor(
                dst_tab[:, :, 3, :], ints[:, 1, :].rearrange("p (r j) -> p r j", j=ROWS), float(ROWS),
                ints[:, 0, :].rearrange("p (r j) -> p r j", j=ROWS), ALU.mult, ALU.add))

            chain = {"at": 0, "n": 0}

            def link_(ins):
                chain["n"] += 1
                ins.then_inc(s_chain, 1)
                dve.wait_ge(s_chain, chain["at"] + chain["n"])

            def compare(ph, i, par, tail):
                p = edge_parts(tail)
                dve.wait_ge(*this(ph["mv_ready"], par, i))
                dve.wait_ge(*this(ph["row_loaded"], par, i, 16))
                dve.wait_ge(*two_ago(ph["summed"], par, i))
                row = irow[0:p, par, 0:p * ROWS].rearrange("p (q j) -> p j q", j=ROWS)
                for h in range(2):
                    nc.vector.scalar_tensor_tensor(
                        same[0:p, par, h, 0, 0:p], row[:, 2 * h, :], cols[0:p, par, 0, 2 * h:2 * h + 1],
                        order[0:p, 1, 0:p], ALU.is_equal, ALU.mult, accum_out=count[0:p, par, 2 * h:2 * h + 1])
                    ins = nc.vector.scalar_tensor_tensor(
                        same[0:p, par, h, 1:3, 0:p], row[:, 2 * h:2 * h + 2, :],
                        cols[0:p, par, 0, 2 * h + 1:2 * h + 2], order[0:p, :, 0:p], ALU.is_equal, ALU.mult,
                        accum_out=count[0:p, par, 2 * h + 1:2 * h + 2])
                link_(ins)
                dve.wait_ge(*two_ago(s_sc1 if ph is A else s_sc2, par, i, 64))
                link_(nc.vector.scalar_tensor_tensor(shift[0:p, par, :], count[0:p, par, :], 1.5,
                                                     cols[0:p, par, 1, :], ALU.is_gt, ALU.mult))
                nc.vector.tensor_tensor(target[0:p, par, :], shift[0:p, par, :], cols[0:p, par, 0, :], ALU.add)\
                    .then_inc(ph["targets"][par], 1)

            def chained(body, per):
                def run(i, par, tail):
                    chain["at"] = done[0] + (2 * i + par) * per
                    chain["n"] = 0
                    body(i, par, tail)
                    assert chain["n"] == per, chain["n"]
                return run

            def body_a(i, par, tail):
                p = edge_parts(tail)
                dve.wait_ge(*(this(A["x_loaded"], par, i, 16) if not tail else (A["x_loaded"][0], 16 * (IT + 2))))
                for c, q in chunk_parts(tail):
                    nc.vector.bn_stats(st6[0:q, par, ROWS + c, :], xin[0:q, par, c, :])
                dve.wait_ge(*this(A["rows_loaded"], par, i, 64))
                for j in range(ROWS):
                    ins = nc.vector.bn_stats(st6[0:p, par, j, :], rows[0:p, par, j, :])
                link_(ins)
                nc.vector.tensor_copy(cols[:, par, :, :], dst_tab[:, 2 * i + par, :, :])
                for c, q in chunk_parts(tail):
                    nc.vector.bn_aggr(mv[0:q, par, ROWS + c, :], st6[0:q, par, ROWS + c, :])
                for j in range(ROWS):
                    ins = nc.vector.bn_aggr(mv[0:p, par, j, :], st6[0:p, par, j, :])
                ins.then_inc(A["mv_ready"][par], 1)
                compare(A, i, par, tail)
                dve.wait_ge(*last(A["hot_used"], par, i))
                for j in range(ROWS):
                    nc.vector.tensor_scalar(hotp[0:p, j, :], iota_p[0:p, :], cols[0:p, par, 2, j:j + 1], None,
                                            ALU.is_equal)
                    ins = nc.vector.tensor_scalar(hotc[0:p, j, :], iota_c[0:p, :], cols[0:p, par, 3, j:j + 1], None,
                                                  ALU.is_equal)
                ins.then_inc(A["hot_ready"][par], 1)
                dve.wait_ge(*this(A["sd_ready"], par, i))
                dve.wait_ge(*two_ago(A["h_ready"], par, i))
                link_(nc.vector.reciprocal(rs[:, par, :], sd[:, par, :]))
                nc.vector.scalar_tensor_tensor(nm[:, par, :], mv[:, par, 0:ROWS, 0], -1.0, rs[:, par, 0:ROWS],
                                               ALU.mult, ALU.mult).then_inc(A["nm_ready"][par], 1)
                normalise(A, i, par, tail)
                dve.wait_ge(*this(A["product"], par, i))
                dve.wait_ge(*two_ago(A["stored"], par, i, 16))
                for c, q in pieces(tail):
                    ins = nc.vector.tensor_tensor(flat(res, par, c, q), psQ[0:q, c, :].rearrange("p c d -> p (c d)"),
                                                  flat(xin, par, c, q), ALU.add)
                ins.then_inc(A["added"][par], 1)

            def normalise(ph, i, par, tail):
                t = xin if ph is A else res
                dve.wait_ge(*two_ago(ph["transposed"], par, i))
                for c, q in chunk_parts(tail):
                    ins = nc.vector.tensor_scalar(aux[0:q, par, c, :], t[0:q, par, c, :],
                                                  mv[0:q, par, ROWS + c, 0:1], rs[0:q, par, ROWS + c:ROWS + c + 1],
                                                  ALU.subtract, ALU.mult)
                ins.then_inc(ph["normed"][par], 1)

            run_a = chained(body_a, 4)
            rounds(dve, run_a)
            run_a(IT, 0, True)
            done[0] += (RF + 1) * 4
            dve.wait_ge(*this(A["hot_used"], 0, IT))
            link(nc.vector.tensor_scalar(rdeg[:, :], psH, 1.0, None, ALU.max))
            link(nc.vector.reciprocal(rdeg[:, :], rdeg[:, :]))

            def body_b(i, par, tail):
                r = 2 * i + par
                dve.wait_ge(*(this(B["x_loaded"], par, i, 16) if not tail else (B["x_loaded"][0], 16 * (IT + 2))))
                dve.wait_ge(*(this(B["a_loaded"], par, i, 16) if not tail else (B["a_loaded"][0], 16 * (IT + 2))))
                dve.wait_ge(*two_ago(B["stored"], par, i, 16))
                link_(nc.vector.tensor_copy(rd[:, par, :], rdeg[:, bass.ds(r * CHUNKS, CHUNKS)]))
                for c, q in chunk_parts(tail):
                    ins = nc.vector.scalar_tensor_tensor(res[0:q, par, c, :], aux[0:q, par, c, :],
                                                         rd[0:q, par, c:c + 1], xin[0:q, par, c, :],
                                                         ALU.mult, ALU.add)
                ins.then_inc(B["added"][par], 1)
                dve.wait_ge(*this(B["added"], par, i))
                for c, q in chunk_parts(tail):
                    ins = nc.vector.bn_stats(st6[0:q, par, ROWS + c, :], res[0:q, par, c, :])
                link_(ins)
                nc.vector.tensor_copy(cols[:, par, 0:2, :], src_tab[:, r, :, :])
                for c, q in chunk_parts(tail):
                    ins = nc.vector.bn_aggr(mv[0:q, par, ROWS + c, :], st6[0:q, par, ROWS + c, :])
                ins.then_inc(B["mv_ready"][par], 1)
                compare(B, i, par, tail)
                dve.wait_ge(*this(B["sd_ready"], par, i))
                link_(nc.vector.reciprocal(rs[:, par, :], sd[:, par, :]))
                normalise(B, i, par, tail)

            run_b = chained(body_b, 5)
            rounds(dve, run_b)
            run_b(IT, 0, True)
            done[0] += (RF + 1) * 5

            def z_of(i, par, c, p, spill):
                if spill:
                    return zs[:, par, c, 0:p]
                return zT[:, 2 * i + par, :].rearrange("p (c q) -> p c q", q=P)[:, c, 0:p]

            def bn_count(i, par, tail, spill):
                for n in range(2):
                    p = NODE_TAIL[n] if tail else P
                    c = slice(n * ROWS, (n + 1) * ROWS)
                    ins = nc.vector.bn_stats(bst[:, bass.ds((2 * i + par) * 2 + n, 1), :].rearrange("p a s -> p (a s)"),
                                             z_of(i, par, c, p, spill))
                return ins

            def body_c(spill):
                def body(i, par, tail):
                    dve.wait_ge(*this(C["transposed"], par, i))
                    if spill:
                        dve.wait_ge(C["z_loaded"][par], (i - KEPT + 1) * 16 + (16 if tail else 0))
                    for c, p in pieces(tail):
                        t = z_of(i, par, c, p, spill)
                        ins = nc.vector.tensor_tensor(t, ps2[par][:, c, 0:p], t, ALU.add)
                    ins.then_inc(C["added"][par], 1)
                return body

            def count_c(spill):
                def body(i, par, tail):
                    dve.wait_ge(*this(C["silu"], par, i))
                    bn_count(i, par, tail, spill).then_inc(C["stats"][par], 1)
                return body

            def pipelined(first, second):
                first(False)(0, 0, False)
                with dve.Fori(0, KEPT - 1) as i:
                    first(False)(i, 1, False)
                    second(False)(i, 0, False)
                    first(False)(i + 1, 0, False)
                    second(False)(i, 1, False)
                first(False)(KEPT - 1, 1, False)
                second(False)(KEPT - 1, 0, False)
                if KEPT < IT:
                    first(True)(KEPT, 0, False)
                    second(False)(KEPT - 1, 1, False)
                    with dve.Fori(KEPT, IT - 1) as i:
                        first(True)(i, 1, False)
                        second(True)(i, 0, False)
                        first(True)(i + 1, 0, False)
                        second(True)(i, 1, False)
                    first(True)(IT - 1, 1, False)
                    second(True)(IT - 1, 0, False)
                first(True)(IT, 0, True)
                second(KEPT < IT)(IT - 1, 1, False)
                second(True)(IT, 0, True)

            pipelined(body_c, count_c)

            def fold(k, sems):
                dve.wait_ge(*this(sems, 1, IT - 1))
                dve.wait_ge(*this(sems, 0, IT))
                nc.vector.bn_aggr(bn[:, k, 0:2], bst[:, :, :].rearrange("p a s -> p (a s)")).then_inc(s_bn[k], 1)
                dve.wait_ge(s_bn[k], 2)
                nc.vector.reciprocal(bn[:, k, 3:4], bn[:, k, 2:3]).then_inc(s_bn[k], 1)
                dve.wait_ge(s_bn[k], 3)
                nc.vector.tensor_tensor(bn[:, k, 4:5], bn[:, k, 3:4], vecs[:, 3 * k + 1:3 * k + 2], ALU.mult)\
                    .then_inc(s_bn[k], 1)
                dve.wait_ge(s_bn[k], 4)
                nc.vector.tensor_tensor(bn[:, k, 5:6], bn[:, k, 4:5], bn[:, k, 0:1], ALU.mult).then_inc(s_bn[k], 1)
                dve.wait_ge(s_bn[k], 5)
                nc.vector.tensor_tensor(bn[:, k, 6:7], vecs[:, 3 * k + 2:3 * k + 3], bn[:, k, 5:6], ALU.subtract)\
                    .then_inc(s_bn[k], 1)

            dve.wait_ge(s_w, 16 * 13)
            fold(0, C["stats"])
            nc.vector.tensor_scalar(w2s[:, :], w2[:, :], bn[:, 0, 4:5], None, ALU.mult).then_inc(s_bn[0], 1)
            dve.wait_ge(s_bw, 1)
            nc.vector.tensor_tensor(bn[:, 0, 7:8], psB[:, 0:1], vecs[:, 3:4], ALU.add).then_inc(s_bn[0], 1)

            def count_f(spill):
                def body(i, par, tail):
                    dve.wait_ge(*this(F["silu"], par, i))
                    bn_count(i, par, tail, spill).then_inc(F["stats"][par], 1)
                return body

            rounds(dve, count_f(False), 0, KEPT)
            rounds(dve, count_f(True), KEPT, IT)
            count_f(True)(IT, 0, True)
            fold(1, F["stats"])

            def finish(i, par, tail):
                dve.wait_ge(*this(G["product"], par, i))
                dve.wait_ge(*this(G["biased"], par, i))
                dve.wait_ge(*two_ago(G["stored"], par, i, 16))
                for c, q in pieces(tail):
                    ins = nc.vector.tensor_tensor(flat(res, par, c, q),
                                                  ps2[par][0:q, c, :].rearrange("p c d -> p (c d)"),
                                                  flat(xin, par, c, q), ALU.add)
                ins.then_inc(G["done"][par], 1)

            rounds(dve, finish)
            finish(IT, 0, True)

        @block.tensor
        def _(pe):
            pe.wait_ge(s_const, 5)
            pe.wait_ge(s_w, 16 * 13)
            pe.wait_ge(s_z0, 1)
            nc.tensor.matmul(psH, hotc[:, 0, 0:P], hotc[:, 0, :], start=True, stop=False).then_inc(s_z0, 1)

            def transposes(t, ps_t, par, tail):
                for c, p in chunk_parts(tail):
                    ins = nc.tensor.transpose(ps_t[:, c, 0:p], t[0:p, par, c, :], ident[0:p, 0:p])
                return ins

            def presum(t, par, tail):
                p = edge_parts(tail)
                for h in range(2):
                    nc.tensor.matmul(psA[:, 2 * h:2 * h + 2, 0:p], t[0:p, par, 2 * h + 1, :],
                                     same[0:p, par, h, 1:3, 0:p], start=True, stop=False)
                    ins = nc.tensor.matmul(psA[:, 2 * h, 0:p], t[0:p, par, 2 * h, :],
                                           same[0:p, par, h, 0, 0:p], start=False, stop=True)
                return ins

            def edge_product(w, par, tail):
                p = edge_parts(tail)
                for j in range(ROWS):
                    ins = nc.tensor.matmul(psV[0:p, j, :], sumT[:, par, j, 0:p], w[:, :], start=True, stop=True)
                return ins

            def round_a(i, par, tail):
                p = edge_parts(tail)
                pe.wait_ge(*this(A["hot_ready"], par, i))
                for j in range(ROWS):
                    ins = nc.tensor.matmul(psH, hotp[0:p, j, :], hotc[0:p, j, :], start=False,
                                           stop=bool(tail and j == ROWS - 1))
                ins.then_inc(A["hot_used"][par], 1)
                pe.wait_ge(*this(A["normed"], par, i))
                pe.wait_ge(*last(A["relu"], par, i))
                transposes(aux, psR, par, tail).then_inc(A["transposed"][par], 1)
                pe.wait_ge(*this(A["h_ready"], par, i))
                pe.wait_ge(*this(A["targets"], par, i))
                pe.wait_ge(*last(A["sum_copied"], par, i))
                presum(hE, par, tail).then_inc(A["summed"][par], 1)
                pe.wait_ge(*this(A["relu"], par, i))
                pe.wait_ge(*last(A["added"], par, i))
                for c, q in chunk_parts(tail):
                    ins = nc.tensor.matmul(psQ[0:q, c, :], hT[:, par, c, 0:q], wr[:, :], start=True, stop=True)
                ins.then_inc(A["product"][par], 1)
                pe.wait_ge(*this(A["sum_copied"], par, i))
                pe.wait_ge(*last(A["v_copied"], par, i))
                edge_product(wl, par, tail).then_inc(A["v_ready"][par], 1)

            rounds(pe, round_a)
            round_a(IT, 0, True)

            def round_b(i, par, tail):
                pe.wait_ge(*this(B["rows_loaded"], par, i, 16))
                pe.wait_ge(*this(B["targets"], par, i))
                pe.wait_ge(*last(B["sum_copied"], par, i))
                presum(rows, par, tail).then_inc(B["summed"][par], 1)
                pe.wait_ge(*this(B["normed"], par, i))
                pe.wait_ge(*last(B["relu"], par, i))
                transposes(aux, psR, par, tail).then_inc(B["transposed"][par], 1)
                pe.wait_ge(*this(B["relu"], par, i))
                pe.wait_ge(*last(B["z_copied"], par, i))
                for n in range(2):
                    q = NODE_TAIL[n] if tail else P
                    c = slice(n * ROWS, (n + 1) * ROWS)
                    ins = nc.tensor.matmul(psQ[:, c, 0:q], w1a[:, :], hT[:, par, c, 0:q], start=True, stop=True)
                ins.then_inc(B["product"][par], 1)
                pe.wait_ge(*this(B["sum_copied"], par, i))
                pe.wait_ge(*last(B["v_copied"], par, i))
                edge_product(w1b, par, tail).then_inc(B["v_ready"][par], 1)

            rounds(pe, round_b)
            round_b(IT, 0, True)

            def round_c(i, par, tail):
                pe.wait_ge(*(this(C["loaded"], par, i, 16) if not tail else (C["loaded"][0], 16 * (IT + 2))))
                pe.wait_ge(*two_ago(C["added"], par, i))
                transposes(xin, ps2[par], par, tail).then_inc(C["transposed"][par], 1)

            pe.wait_ge(*this(B["relu"], 0, IT))
            pe.wait_ge(*this(B["z_copied"], 0, IT))
            rounds(pe, round_c)
            round_c(IT, 0, True)

            pe.wait_ge(s_bn[0], 7)
            nc.tensor.matmul(psB[:, 0:1], w2[:, :], bn[:, 0, 6:7], start=True, stop=True).then_inc(s_bw, 1)

            def round_f(spill):
                def body(i, par, tail):
                    pe.wait_ge(*two_ago(F["silu"], par, i))
                    if spill:
                        pe.wait_ge(F["z_loaded"][par], (i - KEPT + 1) * 16 + (16 if tail else 0))
                    for n in range(2):
                        q = NODE_TAIL[n] if tail else P
                        c = slice(n * ROWS, (n + 1) * ROWS)
                        t = zs[:, par, c, 0:q] if spill else \
                            zT[:, 2 * i + par, :].rearrange("p (c q) -> p c q", q=P)[:, c, 0:q]
                        ins = nc.tensor.matmul(ps2[par][:, c, 0:q], w2s[:, :], t, start=True, stop=True)
                    ins.then_inc(F["product"][par], 1)
                return body

            rounds(pe, round_f(False), 0, KEPT)
            rounds(pe, round_f(True), KEPT, IT)
            round_f(True)(IT, 0, True)

            def round_g(i, par, tail):
                pe.wait_ge(*this(G["scaled"], par, i))
                pe.wait_ge(*two_ago(G["done"], par, i))
                for c, q in chunk_parts(tail):
                    ins = nc.tensor.matmul(ps2[par][0:q, c, :], hT[:, par, c, 0:q], w3[:, :], start=True, stop=True)
                ins.then_inc(G["product"][par], 1)

            pe.wait_ge(*this(F["silu"], 0, IT))
            pe.wait_ge(*this(F["silu"], 1, IT - 1))
            rounds(pe, round_g)
            round_g(IT, 0, True)


_ARGS = ["x", "src", "dst", "edge_attr_128", "L0_gnn_W_l", "L0_gnn_W_r", "L1_gnn_W1", "L1_gnn_b1", "L1_gnn_g1",
         "L1_gnn_be1", "L1_gnn_W2", "L1_gnn_b2", "L1_gnn_g2", "L1_gnn_be2", "L1_gnn_W3", "L1_gnn_b3"]


def kernel(**inputs):
    import numpy as _np
    import concourse.bacc as _bacc
    from concourse import mybir as _mybir
    from concourse.bass_utils import run_bass_kernel_spmd as _run

    nc = _bacc.Bacc("TRN2", target_bir_lowering=False, num_devices=1)
    arrays, args = {}, []
    for name in _ARGS:
        a = _np.asarray(inputs[name])
        if name in ("L0_gnn_W_l", "L0_gnn_W_r"):
            a = a.T
        a = _np.ascontiguousarray(a)
        arrays[f"in_{name}_dram"] = a
        args.append(nc.dram_tensor(f"in_{name}_dram", a.shape, _mybir.dt.from_np(a.dtype), kind="ExternalInput").ap())
    shape = tuple(inputs["x"].shape)
    args.append(nc.dram_tensor("out_0_dram", shape, _mybir.dt.float32, kind="ExternalOutput").ap())
    gnn_layers(nc, *args)
    r = _run(nc, [arrays], core_ids=[0])
    return r.results[0]["out_0_dram"]
```

```python
from contextlib import ExitStack

import concourse.bass as bass
from concourse import mybir

P = 128
ROWS = 4
GROUP = P * ROWS
CHUNKS = 2 * ROWS
ROUND = 2 * GROUP


def this(sem, par, i, inc=1):
    return sem[par], (i + 1) * inc


def two_ago(sem, par, i, inc=1):
    return sem[par], i * inc


def last(sem, par, i, inc=1):
    return sem[1 - par], (i + par) * inc


def gnn_layers(nc, x, src, dst, edge_attr, WlT, WrT, W1, b1, g1, be1, W2, b2, g2, be2, W3, b3, out):
    fp32 = mybir.dt.float32
    fp16 = mybir.dt.float16
    i32 = mybir.dt.int32
    u32 = mybir.dt.uint32
    ALU = mybir.AluOpType
    ACT = mybir.ActivationFunctionType

    N, D = x.shape
    E = src.shape[0]
    EPS = 1e-5
    ACT_A = 6

    RF = N // ROUND
    IT = RF // 2
    NODE_TAIL = [P, (N - RF * ROUND - GROUP) // ROWS]
    EDGE_TAIL = (E - RF * GROUP) // ROWS
    assert RF % 2 == 0 and E // GROUP == RF and GROUP + NODE_TAIL[1] * ROWS == N - RF * ROUND
    assert EDGE_TAIL * ROWS == E - RF * GROUP and 0 < EDGE_TAIL <= P and 0 < NODE_TAIL[1] <= P
    KEPT = 16
    KEPT_LATER = 21
    SPILLED = IT - KEPT
    assert 3 <= SPILLED <= KEPT < KEPT_LATER == IT - 3 and KEPT_LATER % 2 == 1
    FETCHED = 2 * (KEPT_LATER - KEPT)
    assert FETCHED == 1 + (KEPT_LATER - 3) // 2
    ACC_ROWS = 3 * P * -(-(N + GROUP) // (3 * P))
    ZPARTS = 12
    ZREP = 2
    ZCOLS = ACC_ROWS * D // P // RF // ZREP
    assert ZCOLS * RF * ZREP * P == ACC_ROWS * D and RF == 4 * ZPARTS
    COLS = (RF + 1) * CHUNKS

    def node_rows(t):
        full = t[0:RF * ROUND, :].rearrange("(r n p j) d -> r p n (j d)", n=2, p=P, j=ROWS)
        a = t[RF * ROUND:RF * ROUND + GROUP, :].rearrange("(p j) d -> p (j d)", j=ROWS)
        b = t[RF * ROUND + GROUP:N, :].rearrange("(p j) d -> p (j d)", j=ROWS)
        return full, (a, b)

    def edge_cols(t):
        return (t[0:RF * GROUP].rearrange("(r p j) -> r p j", p=P, j=ROWS),
                t[RF * GROUP:E].rearrange("(p j) -> p j", j=ROWS))

    acc1 = nc.dram_tensor("acc1", (ACC_ROWS, D), fp32).ap()
    acc2 = nc.dram_tensor("acc2", (ACC_ROWS, D), fp32).ap()
    y_dram = nc.dram_tensor("y_dram", (N, D), fp32).ap()
    x1_dram = nc.dram_tensor("x1_dram", (N, D), fp32).ap()
    z_dram = nc.dram_tensor("z_dram", (RF - 2 * KEPT + 1, P, ROUND), fp32).ap()
    zz_dram = nc.dram_tensor("zz_dram", (RF - 2 * KEPT_LATER + 1, P, ROUND), fp32).ap()
    zy_dram = nc.dram_tensor("zy_dram", (RF - 2 * KEPT_LATER + 1, P, ROUND), fp32).ap()

    x_v, y_v, x1_v, out_v = (node_rows(t) for t in (x, y_dram, x1_dram, out))
    acc1_v, acc2_v = node_rows(acc1[0:N, :]), node_rows(acc2[0:N, :])
    src_v, dst_v = edge_cols(src), edge_cols(dst)
    src_row = src[0:RF * GROUP].rearrange("(r k) -> r k", k=GROUP)
    dst_row = dst[0:RF * GROUP].rearrange("(r k) -> r k", k=GROUP)
    ea_v = (edge_attr[0:RF * GROUP, :].rearrange("(r p j) d -> r p (j d)", p=P, j=ROWS),
            edge_attr[RF * GROUP:E, :].rearrange("(p j) d -> p (j d)", j=ROWS))
    acc1_z = acc1.rearrange("(p r) d -> p (r d)", p=P).rearrange("p (k a c) -> k p a c", k=ZPARTS, c=ZCOLS)
    acc2_z = acc2.rearrange("(p r) d -> p (r d)", p=P).rearrange("p (k a c) -> k p a c", k=RF, c=ZCOLS)

    def column(t):
        return t.rearrange("(p a) -> p a", a=1)

    ctx = ExitStack()
    with ctx:
        def sb(name, shape, dt=fp32):
            return ctx.enter_context(nc.sbuf_tensor(name, shape, dt))

        def sem(name):
            return ctx.enter_context(nc.semaphore(name))

        def pair(name):
            return [sem(f"{name}_{k}") for k in range(2)]

        wl = sb("wl", [P, D]); wr = sb("wr", [P, D]); w1a = sb("w1a", [P, D]); w1b = sb("w1b", [P, D])
        w2 = sb("w2", [P, D]); w3 = sb("w3", [P, D]); w2s = sb("w2s", [P, D])
        b3b = sb("b3b", [P, D])
        vecs = sb("vecs", [P, 6])
        ident = sb("ident", [P, P])
        eps = sb("eps", [P, 1])
        iota_p = sb("iota_p", [P, P], fp16)
        warm = sb("warm", [P, 1])
        zeros = sb("zeros", [P, ZCOLS])
        dump = sb("dump", [P, ROWS])
        dst_tab = sb("dst_tab", [P, RF + 1, 4, ROWS])
        src_tab = sb("src_tab", [P, RF + 1, 2, ROWS])
        rdeg = sb("rdeg", [P, COLS])
        xin = sb("xin", [P, 2, CHUNKS, D])
        zT = sb("zT", [P, 2 * KEPT_LATER, ROUND])
        zflat = zT[:, :, :].rearrange("p r c -> p (r c)")
        taken = [2 * KEPT * ROUND]

        def part(shape, dt=fp32):
            n = 1
            for k in shape[1:]:
                n *= k
            at = taken[0]
            taken[0] += n
            assert taken[0] <= 2 * KEPT_LATER * ROUND
            t = zflat[:, at:at + n]
            if dt is not fp32:
                t = t.bitcast(dt)
            names = "abcd"[:len(shape) - 1]
            sizes = dict(zip(names, shape[1:]))
            return t.rearrange(f"p ({' '.join(names)}) -> p {' '.join(names)}", **sizes)

        order = part([P, ROWS, P])
        aux = part([P, 2, CHUNKS, D])
        table_ints = aux[:, :, :, :].rearrange("p a c d -> p (a c d)").bitcast(i32)
        IC = (RF + 1) * ROWS
        raw = table_ints[:, 0:2 * IC].rearrange("p (k c) -> p k c", k=2)
        ints = table_ints[:, 2 * IC:4 * IC].rearrange("p (k c) -> p k c", k=2)
        res = sb("res", [P, 2, CHUNKS, D])
        hT = sb("hT", [P, 2, CHUNKS, P])
        rows = part([P, 2, ROWS, D])
        hE = part([P, 2, ROWS, D])
        normed_b = hE[:, :, :, :].rearrange("p a j d -> p (a j) d")
        same = part([P, 2, ROWS * (ROWS + 1) // 2, P])
        hots = same[:, :, :, :].rearrange("p a b c -> p a (b c)").bitcast(fp16)
        hotp = hots[:, :, 0:ROWS * P].rearrange("p a (j c) -> p a j c", j=ROWS)
        hotc = hots[:, :, ROWS * P:ROWS * (P + COLS)].rearrange("p a (j c) -> p a j c", j=ROWS)
        sumT = part([P, ROWS, P])
        vrow = part([P, 2, ROWS, D])
        irow = part([P, 2, GROUP], i32)
        iota_c = part([P, COLS // 2]).bitcast(fp16)
        icol = sb("icol", [P, 2, ROWS], u32)
        cols = part([P, 2, 4, ROWS])
        count = sb("count", [P, 2, ROWS])
        shift = sb("shift", [P, 2, ROWS])
        target = sb("target", [P, 2, ROWS], u32)
        st6 = part([P, 2, 12, 6])
        mv = part([P, 2, 12, 2])
        sd = part([P, 2, 12])
        rs = part([P, 2, 12])
        nm = part([P, 2, 12])
        bst = sb("bst", [P, 2 * (RF + 1), 6])
        bn = sb("bn", [P, 2, 8])

        ps = ctx.enter_context(nc.psum_tensor("ps", [P, 8, 512], fp32))
        psR = ps[:, 0:2, :].rearrange("p b (j c) -> p (b j) c", c=P)
        psQ = ps[:, 2:4, :].rearrange("p b (j c) -> p (b j) c", c=P)
        psA = ps[:, 4, :].rearrange("p (j c) -> p j c", c=P)
        psV = ps[:, 5, :].rearrange("p (j c) -> p j c", c=P)
        psH = ps[:, 6, 0:COLS]
        psB = ps[:, 7, :]
        ps2 = [ps[:, 2 * k:2 * k + 2, :].rearrange("p b (j c) -> p (b j) c", c=P) for k in range(2)]

        s_w = sem("weights_loaded")
        s_idx = sem("indices_loaded")
        s_const = sem("constants_made")
        s_mem = sem("memsets_done")
        s_chain = sem("vector_chain")
        s_tab = sem("tables_made")
        s_zero1 = sem("acc1_zeroed")
        s_zero2 = sem("acc2_zeroed")
        s_turn = sem("pool_turn")
        s_eps = sem("eps_set")

        def phase(tag, names):
            return {k: pair(f"{tag}_{k}") for k in names.split()}

        common = ("row_loaded rows_loaded mv_ready sd_ready act_normed nm_ready targets transposed "
                  "relu product summed sum_copied v_ready v_copied added stored")
        A = phase("a", common + " normed x_loaded icol_loaded h_ready")
        H = phase("h", "ready used")
        B = phase("b", common + " y_loaded a_loaded z_copied z_stored")
        C = phase("c", "transposed added silu stats stored")
        F = phase("f", "product silu stats stored")
        G = phase("g", "scaled product done stored")
        acc2_loaded = [pair(f"acc2_loaded_{k}") for k in range(2)]
        x1_loaded = [pair(f"x1_loaded_{k}") for k in range(2)]
        late_loaded = [sem(f"late_loaded_{r}") for r in range(2 * KEPT_LATER, RF + 1)]
        s_sc1 = pair("acc1_scattered")
        s_sc2 = pair("acc2_scattered")
        s_z0 = sem("hist_opened")
        s_zeros = sem("zeros_made")
        s_fetched = sem("z_fetched")
        s_bn = pair("bn_steps")
        s_bw = sem("bn_bias_product")

        block = ctx.enter_context(nc.Block())

        def pieces(tail):
            return [(slice(0, ROWS), NODE_TAIL[0]), (slice(ROWS, CHUNKS), NODE_TAIL[1])] if tail else \
                [(slice(0, CHUNKS), P)]

        def chunk_parts(tail):
            return [(c, NODE_TAIL[c // ROWS] if tail else P) for c in range(CHUNKS)]

        def edge_parts(tail):
            return EDGE_TAIL if tail else P

        def flat(t, par, c, p):
            return t[0:p, par, c, :].rearrange("p c d -> p (c d)")

        def rounds(eng, body, lo=0, hi=IT):
            if hi > lo:
                for par in range(2):
                    body(lo, par, False)
            if hi > lo + 1:
                with eng.Fori(lo + 1, hi) as i:
                    for par in range(2):
                        body(i, par, False)

        def sweep(eng, body, bounds, wide=False):
            def fixed(r):
                return (r // 2, r % 2, r == RF, sum(b <= r // 2 for b in bounds)) if 0 <= r <= RF else None

            n = 4 if wide else 3

            def peeled(lo, hi):
                for r in range(lo, hi):
                    body(*(fixed(r + k) for k in range(-1, n - 1)))

            at = 0
            for k, (lo, hi) in enumerate(zip((0, *bounds), (*bounds, IT))):
                if hi > lo + 4:
                    peeled(at, 2 * lo + 4)
                    with eng.Fori(lo + 2, hi - 1) as i:
                        near = [(i - 1, 1, False, k), (i, 0, False, k), (i, 1, False, k),
                                (i + 1, 0, False, k), (i + 1, 1, False, k)]
                        body(*near[0:n])
                        body(*near[1:n + 1])
                    at = 2 * hi - 2
            peeled(at, RF + 1)

        def doubled(eng, body, lo, hi):
            assert (hi - lo) % 2 == 0
            with eng.Fori(0, (hi - lo) // 2) as k:
                for q in range(2):
                    for par in range(2):
                        body(2 * k + lo + q, k + (lo + q) // 2, (lo + q) % 2, par)

        def late_rounds():
            return [(r // 2, r % 2, r == RF) for r in range(2 * KEPT_LATER, RF + 1)]

        def late(i, par, tail, times):
            return late_loaded[2 * (i - KEPT_LATER) + par], (32 if tail else 16) * times

        def acc2_pair(i, odd):
            return xin if odd or (type(i) is int and i >= KEPT_LATER) else res

        def z_later(i, par):
            if type(i) is int and i >= KEPT_LATER:
                return (hT if i % 2 else res)[:, par, :, :]
            return kept(i, par)

        def x1_place(i, par):
            if type(i) is int and not 2 <= i < IT - 1:
                return (xin if i in (0, IT - 1) else res)[:, par, :, :]
            return kept(i - 2, par)

        def kept(i, par):
            return zT[:, 2 * i + par, :].rearrange("p (c q) -> p c q", q=P)

        def place_a(i, par, late):
            return (2 * (i - SPILLED) + par, kept(i - SPILLED, par)) if late else \
                (2 * (i + KEPT) + par, kept(i + KEPT - SPILLED, par))

        def round_a_of(i, par, tail, late):
            return RF if tail else place_a(i, par, late)[0]

        def rows_a(i, par, tail, late):
            return xin[:, par, :, :] if tail else place_a(i, par, late)[1]

        def spilled(d, t, tail):
            if not tail:
                return [(d, t.rearrange("p c q -> p (c q)"))]
            d = d.rearrange("f (c q) -> f c q", q=P)
            return [(d[:, c, 0:p], t[:, c, 0:p]) for c, p in pieces(True)]

        @block.sync
        def _(sp):
            sp.wait_ge(s_mem, 1)
            for k, v in enumerate((dst_v, src_v)):
                sp.dma_start(raw[:, k, 0:RF * ROWS].rearrange("p (r j) -> p r j", j=ROWS),
                             v[0].rearrange("r p j -> p r j")).then_inc(s_idx, 16)
                sp.dma_start(raw[0:EDGE_TAIL, k, RF * ROWS:], v[1]).then_inc(s_idx, 16)
            for t, w in ((wl, WlT), (wr, WrT), (w1a, W1[0:D, :]), (w1b, W1[D:2 * D, :]), (w2, W2), (w3, W3)):
                sp.dma_start(t[:, :], w).then_inc(s_w, 16)
            for k, v in enumerate((b1, g1, be1, b2, g2, be2)):
                sp.dma_start(vecs[:, k:k + 1], column(v)).then_inc(s_w, 16)
            sp.dma_start(b3b[:, :], b3.partition_broadcast(P)).then_inc(s_w, 16)

            def load_nodes(t, v, r, tail, sem):
                for n in range(2 if tail else 0):
                    p = NODE_TAIL[n]
                    sp.dma_start(t[0:p, n * ROWS:(n + 1) * ROWS, :].rearrange("p j d -> p (j d)"),
                                 v[1][n]).then_inc(sem, 16)
                if not tail:
                    sp.dma_start(t.rearrange("p (n j) d -> p n (j d)", n=2), v[0][r]).then_inc(sem, 16)

            def store_nodes(t, v, r, tail, sem):
                for n in range(2 if tail else 0):
                    p = NODE_TAIL[n]
                    sp.dma_start(v[1][n], t[0:p, n * ROWS:(n + 1) * ROWS, :].rearrange("p j d -> p (j d)"))\
                        .then_inc(sem, 16)
                if not tail:
                    sp.dma_start(v[0][r], t.rearrange("p (n j) d -> p n (j d)", n=2)).then_inc(sem, 16)

            def load_a(i, par, tail, late):
                r = round_a_of(i, par, tail, late)
                sp.wait_ge(*two_ago(A["rows_loaded"], par, i, 64))
                dst_i, src_i = (dst[RF * GROUP:E], src_v[1]) if tail else (dst_row[r], src_v[0][r])
                p = EDGE_TAIL if tail else P
                sp.dma_start(icol[0:p, par, :], src_i.bitcast(u32)).then_inc(A["icol_loaded"][par], 16)
                sp.wait_ge(*two_ago(A["targets"], par, i))
                sp.dma_start(irow[:, par, 0:p * ROWS], dst_i.partition_broadcast(P))\
                    .then_inc(A["row_loaded"][par], 16)
                sp.wait_ge(*two_ago(A["mv_ready"], par, i))
                load_nodes(rows_a(i, par, tail, late), x_v, r, tail, A["x_loaded"][par])

            def store_a(i, par, tail, late):
                if not tail:
                    sp.dma_start(acc2_z[2 * i + par], zeros[:, :].unsqueeze(1).broadcast_to([P, ZREP, ZCOLS]))\
                        .then_inc(s_zero2, 16)
                if tail or not late:
                    sp.wait_ge(*this(A["added"], par, i))
                    store_nodes(res[:, par, :, :] if tail else rows_a(i, par, tail, late), y_v,
                                round_a_of(i, par, tail, late), tail, A["stored"][par])
                else:
                    sp.wait_ge(A["stored"][par], 16 * SPILLED)

            def step_a(before, now, after, ahead):
                if ahead:
                    load_a(*ahead)
                if before:
                    store_a(*before)

            def all_stored(sems, kept_its):
                sp.wait_ge(sems[0], 16 * (IT - kept_its + 2))
                sp.wait_ge(sems[1], 16 * (IT - kept_its))

            def clear_acc1():
                sp.wait_ge(s_zeros, 1)
                for k in range(ZPARTS):
                    sp.dma_start(acc1_z[k], zeros[:, :].unsqueeze(1).broadcast_to([P, 4 * ZREP, ZCOLS]))\
                        .then_inc(s_zero1, 16)

            load_a(0, 0, False, False)
            load_a(0, 1, False, False)
            clear_acc1()
            sweep(sp, step_a, (SPILLED,), wide=True)
            store_a(IT, 0, True, True)

            def load_b_nodes(i, par, tail, spill):
                r = 2 * i + par
                sp.wait_ge(*two_ago(B["added"], par, i))
                load_nodes(aux[:, par, :, :], acc1_v, r, tail, B["a_loaded"][par])
                if spill:
                    load_nodes(xin[:, par, :, :], y_v, r, tail, B["y_loaded"][par])

            def load_b_edges(i, par, tail, spill):
                r = 2 * i + par
                src_i, ea = (src[RF * GROUP:E], ea_v[1]) if tail else (src_row[r], ea_v[0][r])
                p = EDGE_TAIL if tail else P
                sp.wait_ge(*two_ago(B["targets"], par, i))
                sp.dma_start(irow[:, par, 0:p * ROWS], src_i.partition_broadcast(P))\
                    .then_inc(B["row_loaded"][par], 16)
                sp.wait_ge(*two_ago(B["summed"], par, i))
                sp.dma_start(rows[0:p, par, :, :].rearrange("p j d -> p (j d)"), ea)\
                    .then_inc(B["rows_loaded"][par], 16)

            def step_b(before, now, after, ahead):
                i, par, tail, spill = now
                if ahead:
                    load_b_nodes(*ahead)
                sp.wait_ge(*this(B["added"], par, i))
                store_nodes(res[:, par, :, :], x1_v, 2 * i + par, tail, B["stored"][par])
                if ahead:
                    load_b_edges(*ahead)

            all_stored(A["stored"], KEPT)
            sp.wait_ge(*this(s_sc1, 0, IT, 64))
            sp.wait_ge(*this(s_sc1, 1, IT - 1, 64))
            sp.wait_ge(*this(A["transposed"], 0, IT))
            sp.wait_ge(*this(A["targets"], 0, IT))
            for par in range(2):
                load_b_nodes(0, par, False, 0)
                load_b_edges(0, par, False, 0)
            sweep(sp, step_b, (KEPT,), wide=True)

            sp.wait_ge(*this(s_sc2, 0, IT, 64))
            sp.wait_ge(*this(s_sc2, 1, IT - 1, 64))
            sp.wait_ge(*this(B["stored"], 1, IT - 1, 16))
            sp.wait_ge(B["stored"][0], 16 * (IT + 2))
            all_stored(B["z_stored"], KEPT)

            def load_c(i, odd, par, tail=False):
                load_nodes(acc2_pair(i, odd)[:, par, :, :], acc2_v, 2 * i + par, tail, acc2_loaded[odd][par])

            def reload_c(i, half, odd, par):
                sp.wait_ge(C["transposed"][par], i - 1)
                load_c(i, odd, par)

            def load_late(d, first, i, par, tail, t):
                for a, b in spilled(d[2 * (i - first) + par], t, tail):
                    sp.dma_start(b, a).then_inc(late_loaded[2 * (i - KEPT_LATER) + par], 16)

            def store_z(ph, d, i, par, tail):
                sp.wait_ge(*this(ph["silu"], par, i))
                sp.wait_ge(*this(ph["stats"], par, i))
                for a, b in spilled(d[2 * (i - KEPT_LATER) + par], z_later(i, par), tail):
                    sp.dma_start(a, b).then_inc(ph["stored"][par], 16)

            def fetch(k):
                sp.dma_start(zT[:, 2 * KEPT + k, :], z_dram[k]).then_inc(s_fetched, 16)

            for i in range(2):
                for par in range(2):
                    load_c(i, i % 2, par)
            fetch(0)
            for par in range(2):
                load_late(z_dram, KEPT, KEPT_LATER, par, False, z_later(KEPT_LATER, par))
                reload_c(2, 1, 0, par)
            with sp.Fori(0, (KEPT_LATER - 3) // 2) as k:
                sp.wait_ge(s_fetched, 16 * (k + 1))
                fetch(k + 1)
                for q in range(2):
                    for par in range(2):
                        reload_c(2 * k + 3 + q, k + 1 + q, 1 - q, par)
            for par in range(2):
                reload_c(KEPT_LATER, KEPT_LATER // 2, 1, par)
            for i, par, tail in late_rounds():
                nxt = i + 1 if (i, par) != (IT - 1, 1) else None
                if nxt and nxt <= IT and not (nxt == IT and par):
                    if i == KEPT_LATER:
                        sp.wait_ge(C["transposed"][par], i)
                    else:
                        sp.wait_ge(C["stored"][par], 16 * (i - KEPT_LATER))
                    load_late(z_dram, KEPT, nxt, par, nxt == IT, z_later(nxt, par))
                    sp.wait_ge(*this(C["transposed"], par, i))
                    load_c(nxt, nxt % 2, par, nxt == IT)
                store_z(C, zz_dram, i, par, tail)

            all_stored(C["stored"], KEPT_LATER)
            for i in range(KEPT_LATER, KEPT_LATER + 2):
                for par in range(2):
                    load_late(zz_dram, KEPT_LATER, i, par, False, z_later(i, par))

            def load_x1(i, odd, par, tail=False):
                load_nodes(x1_place(i, par), x1_v, 2 * i + par, tail, x1_loaded[odd][par])

            for par in range(2):
                load_x1(0, 0, par)
            before = None
            for i, par, tail in late_rounds():
                store_z(F, zy_dram, i, par, tail)
                if before and (before[0] + 2, before[1], before[0] + 2 == IT) in late_rounds():
                    j, odd = before[0], before[1]
                    sp.wait_ge(*this(F["stored"], odd, j - KEPT_LATER, 16))
                    load_late(zz_dram, KEPT_LATER, j + 2, odd, j + 2 == IT, z_later(j + 2, odd))
                before = (i, par)

            all_stored(F["stored"], KEPT_LATER)
            for par in range(2):
                load_x1(1, 1, par)

            def store_out(i, par, tail=False):
                sp.wait_ge(*this(G["done"], par, i))
                store_nodes(x1_place(i, par), out_v, 2 * i + par, tail, G["stored"][par])

            def step_g(i, half, odd, par):
                sp.wait_ge(*this(G["scaled"], par, i))
                sp.wait_ge(x1_loaded[odd][par], 16 * (half + 1))
                load_x1(i + 2, odd, par)
                store_out(i, par)

            for i in range(3):
                for par in range(2):
                    step_g(i, i // 2, i % 2, par)
            doubled(sp, step_g, 3, 9)
            for par in range(2):
                sp.wait_ge(G["stored"][par], 16 * 9)
            for i, par, tail in late_rounds():
                load_late(zy_dram, KEPT_LATER, i, par, tail, kept(i - KEPT_LATER, par))
            doubled(sp, step_g, 9, KEPT_LATER)
            for par in range(2):
                sp.wait_ge(x1_loaded[1][par], 16 * (KEPT_LATER // 2 + 1))
                load_x1(IT - 1, 1, par)
                store_out(KEPT_LATER, par)
            sp.wait_ge(x1_loaded[0][0], 16 * (IT // 2))
            load_x1(IT, 0, 0, True)
            for i, par, tail in late_rounds()[2:]:
                store_out(i, par, tail)
            sp.wait_ge(*this(G["stored"], 1, IT - 1, 16))
            sp.wait_ge(G["stored"][0], 16 * (IT + 2))

        @block.gpsimd
        def _(pool):
            nc.gpsimd.memset(raw, 0).then_inc(s_mem, 1)
            nc.gpsimd.memset(ident[:, :], 0.0).then_inc(s_turn, 1)
            nc.gpsimd.memset(order[:, :, :], 1.0).then_inc(s_turn, 1)
            pool.wait_ge(s_turn, 2)
            nc.gpsimd.affine_select(out=ident[:, :], in_=ident[:, :], compare_op=ALU.not_equal, fill=1.0,
                                    base=0, pattern=[[-1, P]], channel_multiplier=1).then_inc(s_const, 1)
            nc.gpsimd.affine_select(out=order[:, ROWS - 1, :], in_=order[:, ROWS - 1, :], compare_op=ALU.is_ge, fill=0.0,
                                    base=0, pattern=[[-1, P]], channel_multiplier=1).then_inc(s_const, 1)
            nc.gpsimd.iota(iota_p[:, :], [[1, P]], base=0, channel_multiplier=0,
                           allow_small_or_imprecise_dtypes=True).then_inc(s_const, 1)
            nc.gpsimd.iota(iota_c[:, :], [[1, COLS]], base=0, channel_multiplier=0,
                           allow_small_or_imprecise_dtypes=True).then_inc(s_const, 1)
            nc.gpsimd.iota(dump[:, :], [[P, ROWS]], base=N, channel_multiplier=1,
                           allow_small_or_imprecise_dtypes=True).then_inc(s_const, 1)

            def hold(s, value):
                pool.wait_ge(s, value)
                pool.sem_inc(s_turn, 1)

            def gather(i, par, tail):
                p = edge_parts(tail)
                hold(*this(A["icol_loaded"], par, i, 16))
                hold(*two_ago(A["h_ready"], par, i))
                for j in range(ROWS):
                    pool.indirect_dma_start(
                        rows[0:p, par, j, :], None, x,
                        bass.IndirectOffsetOnAxis(ap=icol[0:p, par, j:j + 1], axis=0))\
                        .then_inc(A["rows_loaded"][par], 16)

            def scatter(ph, acc, s_sc, i, par, tail):
                p = edge_parts(tail)
                hold(*this(ph["v_copied"], par, i))
                hold(*this(ph["targets"], par, i))
                hold(*last(s_sc, par, i, 64))
                for j in range(ROWS):
                    pool.indirect_dma_start(
                        acc, bass.IndirectOffsetOnAxis(ap=target[0:p, par, j:j + 1], axis=0),
                        vrow[0:p, par, j, :], None, compute_op=ALU.add).then_inc(s_sc[par], 16)

            gather(0, 0, False)
            gather(0, 1, False)
            pool.wait_ge(s_zero1, 16 * ZPARTS)
            for par in range(2):
                gather(1, par, False)
                scatter(A, acc1, s_sc1, 0, par, False)
            with pool.Fori(1, IT - 1) as i:
                for par in range(2):
                    gather(i + 1, par, False)
                    scatter(A, acc1, s_sc1, i, par, False)
            gather(IT, 0, True)
            scatter(A, acc1, s_sc1, IT - 1, 0, False)
            scatter(A, acc1, s_sc1, IT - 1, 1, False)
            scatter(A, acc1, s_sc1, IT, 0, True)
            pool.wait_ge(s_zero2, 16 * RF)
            rounds(pool, lambda i, par, tail: scatter(B, acc2, s_sc2, i, par, tail))
            scatter(B, acc2, s_sc2, IT, 0, True)

        @block.scalar
        def _(act):
            act.wait_ge(s_eps, 1)
            nc.scalar.activation(warm[:, :], eps[:, :], ACT.Sqrt)

            def root(ph, after):
                if after:
                    i, par = after[:2]
                    act.wait_ge(*this(ph["mv_ready"], par, i))
                    nc.scalar.activation(sd[:, par, :], mv[:, par, :, 1], ACT.Sqrt, bias=eps[:, :])\
                        .then_inc(ph["sd_ready"][par], 1)

            def normalise(ph, t, to, i, par, tail, chunks):
                for c, p in chunk_parts(tail)[:chunks]:
                    k = ROWS + c
                    ins = nc.scalar.activation(to[0:p, c, :], t[0:p, c, :], ACT.Identity,
                                               bias=nm[0:p, par, k:k + 1], scale=rs[0:p, par, k:k + 1])
                ins.then_inc(ph["act_normed"][par], 1)

            def relu(ph, i, par, tail):
                act.wait_ge(*this(ph["transposed"], par, i))
                act.wait_ge(*two_ago(ph["product"], par, i))
                for c, p in pieces(tail):
                    ins = nc.scalar.activation(hT[:, par, c, 0:p], psR[:, c, 0:p], ACT.Relu)
                ins.then_inc(ph["relu"][par], 1)

            def copy_sums(ph, i, par, tail):
                p = edge_parts(tail)
                act.wait_ge(*this(ph["summed"], par, i))
                act.wait_ge(*last(ph["v_ready"], par, i))
                nc.scalar.activation(sumT[:, :, 0:p], psA[:, :, 0:p], ACT.Copy)\
                    .then_inc(ph["sum_copied"][par], 1)

            def copy_v(ph, s_sc, i, par, tail):
                p = edge_parts(tail)
                act.wait_ge(*this(ph["v_ready"], par, i))
                act.wait_ge(*two_ago(s_sc, par, i, 64))
                nc.scalar.activation(vrow[0:p, par, :, :], psV[0:p, :, :], ACT.Copy).then_inc(ph["v_copied"][par], 1)

            def body_a(before, now, after):
                i, par, tail, late = now
                p = edge_parts(tail)
                act.wait_ge(*this(A["nm_ready"], par, i))
                act.wait_ge(*two_ago(A["summed"], par, i))
                for j in range(ROWS):
                    ins = nc.scalar.activation(hE[0:p, par, j, :], rows[0:p, par, j, :], ACT.Relu,
                                               bias=nm[0:p, par, j:j + 1], scale=rs[0:p, par, j:j + 1])
                ins.then_inc(A["h_ready"][par], 1)
                act.wait_ge(*two_ago(A["transposed"], par, i))
                normalise(A, rows_a(i, par, tail, late), aux[:, par, :, :], i, par, tail, ACT_A)
                copy_sums(A, i, par, tail)
                relu(A, i, par, tail)
                copy_v(A, s_sc1, i, par, tail)
                root(A, after)

            root(A, (0, 0))
            sweep(act, body_a, (SPILLED,))

            def copy_z(i, par, tail, spill):
                act.wait_ge(*this(B["product"], par, i))
                for c, p in pieces(tail):
                    z = hT[:, par, c, 0:p] if spill else kept(i, par)[:, c, 0:p]
                    ins = nc.scalar.activation(z, psQ[:, c, 0:p], ACT.Copy)
                ins.then_inc(B["z_copied"][par], 1)
                if spill:
                    act.wait_ge(*this(B["z_copied"], par, i))
                    for d, t in spilled(z_dram[2 * (i - KEPT) + par], hT[:, par, :, :], tail):
                        act.dma_start(d, t).then_inc(B["z_stored"][par], 16)

            def body_b(before, now, after):
                i, par, tail, spill = now
                act.wait_ge(*this(B["nm_ready"], par, i))
                act.wait_ge(*last(B["transposed"], par, i))
                normalise(B, res[:, par, :, :], normed_b, i, par, tail, CHUNKS)
                if before:
                    copy_z(*before)
                copy_sums(B, i, par, tail)
                if spill:
                    act.wait_ge(B["z_stored"][par], (i - KEPT) * 16)
                relu(B, i, par, tail)
                root(B, after)
                copy_v(B, s_sc2, i, par, tail)

            act.wait_ge(s_w, 16 * 13)
            root(B, (0, 0))
            sweep(act, body_b, (KEPT,))
            copy_z(IT, 0, True, 1)

            def silu_c(i, par, tail):
                act.wait_ge(*this(C["added"], par, i))
                for c, p in pieces(tail):
                    t = z_later(i, par)[:, c, 0:p]
                    ins = nc.scalar.activation(t, t, ACT.Silu, bias=vecs[:, 0:1])
                ins.then_inc(C["silu"][par], 1)

            nc.scalar.activation(warm[:, :], eps[:, :], ACT.Silu)
            rounds(act, silu_c, 0, KEPT_LATER)
            for r in late_rounds():
                silu_c(*r)

            def bn_root(k):
                act.wait_ge(s_bn[k], 1)
                nc.scalar.activation(bn[:, k, 2:3], bn[:, k, 1:2], ACT.Sqrt, bias=eps[:, :]).then_inc(s_bn[k], 1)

            bn_root(0)
            act.wait_ge(s_bn[0], 8)
            nc.scalar.activation(warm[:, :], eps[:, :], ACT.Silu)

            def silu_f(i, par, tail):
                act.wait_ge(*this(F["product"], par, i))
                for c, p in pieces(tail):
                    ins = nc.scalar.activation(z_later(i, par)[:, c, 0:p], ps2[par][:, c, 0:p], ACT.Silu,
                                               bias=bn[:, 0, 7:8])
                ins.then_inc(F["silu"][par], 1)

            rounds(act, silu_f, 0, KEPT_LATER)
            for r in late_rounds():
                silu_f(*r)
            bn_root(1)
            act.wait_ge(s_bn[1], 6)
            act.wait_ge(F["stored"][0], 16 * (IT - KEPT_LATER + 2))
            act.wait_ge(F["stored"][1], 16 * (IT - KEPT_LATER))

            def scale_g(i, par, tail):
                is_late = type(i) is int and i >= KEPT_LATER
                if is_late:
                    act.wait_ge(*late(i, par, tail, 3))
                act.wait_ge(*two_ago(G["product"], par, i))
                z = kept(i - KEPT_LATER if is_late else i, par)
                for c, p in pieces(tail):
                    ins = nc.scalar.activation(hT[:, par, c, 0:p], z[:, c, 0:p], ACT.Identity,
                                               bias=bn[:, 1, 6:7], scale=bn[:, 1, 4:5])
                ins.then_inc(G["scaled"][par], 1)

            rounds(act, scale_g, 0, KEPT_LATER)
            for r in late_rounds():
                scale_g(*r)

        @block.vector
        def _(dve):
            done = [0]

            def link(ins):
                done[0] += 1
                ins.then_inc(s_chain, 1)
                dve.wait_ge(s_chain, done[0])

            nc.vector.memset(eps[:, :], EPS).then_inc(s_eps, 1)
            nc.vector.memset(zeros[:, :], 0.0).then_inc(s_zeros, 1)
            nc.vector.memset(hots, 0.0).then_inc(s_z0, 1)
            link(nc.vector.memset(mv[:, :, :, :], 1.0))
            dve.wait_ge(s_z0, 2)
            dve.wait_ge(s_idx, 64)
            dve.wait_ge(s_const, 5)
            for k, tab in enumerate((dst_tab, src_tab)):
                r3 = raw[:, k, :].rearrange("p (r j) -> p r j", j=ROWS)
                link(nc.vector.tensor_copy(tab[:, :, 0, :], r3))
                for j in range(ROWS):
                    ins = nc.vector.tensor_scalar(tab[:, :, 1, j], tab[:, :, 0, j], -1.0, dump[:, j:j + 1],
                                                  ALU.mult, ALU.add)
                link(ins)
            link(nc.vector.tensor_scalar(ints[:, 0, :], raw[:, 0, :], 2, P - 1, ALU.logical_shift_right,
                                         ALU.bitwise_and))
            nc.vector.tensor_copy(dst_tab[:, :, 2, :], ints[:, 0, :].rearrange("p (r j) -> p r j", j=ROWS))
            link(nc.vector.tensor_scalar(ints[:, 1, :], raw[:, 0, :], 9, None, ALU.logical_shift_right))
            link(nc.vector.tensor_scalar(ints[:, 0, :], raw[:, 0, :], ROWS - 1, None, ALU.bitwise_and))
            link(nc.vector.scalar_tensor_tensor(
                dst_tab[:, :, 3, :], ints[:, 1, :].rearrange("p (r j) -> p r j", j=ROWS), float(ROWS),
                ints[:, 0, :].rearrange("p (r j) -> p r j", j=ROWS), ALU.mult, ALU.add))

            chain = {"at": 0, "n": 0}

            def link_(ins):
                chain["n"] += 1
                ins.then_inc(s_chain, 1)
                dve.wait_ge(s_chain, chain["at"] + chain["n"])

            def compare(ph, i, par, tail):
                p = edge_parts(tail)
                dve.wait_ge(*this(ph["mv_ready"], par, i))
                dve.wait_ge(*this(ph["row_loaded"], par, i, 16))
                dve.wait_ge(*two_ago(ph["summed"], par, i))
                row = irow[0:p, par, 0:p * ROWS].rearrange("p (q j) -> p j q", j=ROWS)
                for j in range(ROWS):
                    at = j * (j + 1) // 2
                    ins = nc.vector.scalar_tensor_tensor(
                        same[0:p, par, at:at + j + 1, 0:p], row[:, 0:j + 1, :], cols[0:p, par, 0, j:j + 1],
                        order[0:p, ROWS - 1 - j:ROWS, 0:p], ALU.is_equal, ALU.mult,
                        accum_out=count[0:p, par, j:j + 1])
                link_(ins)
                dve.wait_ge(*two_ago(s_sc1 if ph is A else s_sc2, par, i, 64))
                link_(nc.vector.scalar_tensor_tensor(shift[0:p, par, :], count[0:p, par, :], 1.5,
                                                     cols[0:p, par, 1, :], ALU.is_gt, ALU.mult))
                nc.vector.tensor_tensor(target[0:p, par, :], shift[0:p, par, :], cols[0:p, par, 0, :], ALU.add)\
                    .then_inc(ph["targets"][par], 1)

            def chained(body, per):
                def run(before, now, after):
                    chain["at"] = done[0] + (2 * now[0] + now[1]) * per
                    chain["n"] = 0
                    body(before, now, after)
                    assert chain["n"] == per, chain["n"]
                return run

            def histogram(i, par, tail):
                p = edge_parts(tail)
                dve.wait_ge(*two_ago(H["used"], par, i))
                chain["at"], chain["n"] = done[0] + 2 * i + par, 0
                link_(nc.vector.tensor_copy(cols[:, par, :, :], dst_tab[:, 2 * i + par, :, :]))
                for j in range(ROWS):
                    nc.vector.tensor_scalar(hotp[0:p, par, j, :], iota_p[0:p, :], cols[0:p, par, 2, j:j + 1], None,
                                            ALU.is_equal)
                    ins = nc.vector.tensor_scalar(hotc[0:p, par, j, :], iota_c[0:p, :], cols[0:p, par, 3, j:j + 1],
                                                  None, ALU.is_equal)
                ins.then_inc(H["ready"][par], 1)

            rounds(dve, histogram)
            histogram(IT, 0, True)
            done[0] += RF + 1
            dve.wait_ge(*this(H["used"], 0, IT))
            link(nc.vector.tensor_scalar(rdeg[:, :], psH, 1.0, None, ALU.max))
            link(nc.vector.reciprocal(rdeg[:, :], rdeg[:, :]))

            def scales(ph, i, par):
                dve.wait_ge(*this(ph["sd_ready"], par, i))
                link_(nc.vector.reciprocal(rs[:, par, :], sd[:, par, :]))
                link_(nc.vector.scalar_tensor_tensor(nm[:, par, :], mv[:, par, :, 0], -1.0, rs[:, par, :],
                                                     ALU.mult, ALU.mult))
                dve.sem_inc(ph["nm_ready"][par], 1)

            def add_a(i, par, tail, late):
                dve.wait_ge(*this(A["product"], par, i))
                x_t = rows_a(i, par, tail, late)
                y_t = res[:, par, :, :] if tail else x_t
                for c, q in pieces(tail):
                    ins = nc.vector.tensor_tensor(y_t[0:q, c, :], psQ[0:q, c, :], x_t[0:q, c, :], ALU.add)
                ins.then_inc(A["added"][par], 1)

            def body_a(before, now, after):
                i, par, tail, late = now
                p = edge_parts(tail)
                dve.wait_ge(*((A["x_loaded"][0], 16 * (IT + 2)) if tail else this(A["x_loaded"], par, i, 16)))
                x_t = rows_a(i, par, tail, late)
                for c, q in chunk_parts(tail):
                    nc.vector.bn_stats(st6[0:q, par, ROWS + c, :], x_t[0:q, c, :])
                dve.wait_ge(*this(A["rows_loaded"], par, i, 64))
                for j in range(ROWS):
                    ins = nc.vector.bn_stats(st6[0:p, par, j, :], rows[0:p, par, j, :])
                link_(ins)
                nc.vector.tensor_copy(cols[:, par, :, :], dst_tab[:, round_a_of(i, par, tail, late), :, :])
                for c, q in chunk_parts(tail):
                    nc.vector.bn_aggr(mv[0:q, par, ROWS + c, :], st6[0:q, par, ROWS + c, :])
                for j in range(ROWS):
                    ins = nc.vector.bn_aggr(mv[0:p, par, j, :], st6[0:p, par, j, :])
                ins.then_inc(A["mv_ready"][par], 1)
                compare(A, i, par, tail)
                dve.wait_ge(*two_ago(A["h_ready"], par, i))
                dve.wait_ge(*two_ago(A["act_normed"], par, i))
                scales(A, i, par)
                dve.wait_ge(*two_ago(A["transposed"], par, i))
                for c, q in chunk_parts(tail)[ACT_A:]:
                    k = ROWS + c
                    ins = nc.vector.tensor_scalar(aux[0:q, par, c, :], x_t[0:q, c, :], mv[0:q, par, k, 0:1],
                                                  rs[0:q, par, k:k + 1], ALU.subtract, ALU.mult)
                ins.then_inc(A["normed"][par], 1)
                if before:
                    add_a(*before)

            sweep(dve, chained(body_a, 5), (SPILLED,))
            add_a(IT, 0, True, True)
            done[0] += (RF + 1) * 5

            def body_b(before, now, after):
                i, par, tail, spill = now
                r = 2 * i + par
                if spill:
                    dve.wait_ge(B["y_loaded"][par], (i - KEPT + 1) * 16 + (16 if tail else 0))
                dve.wait_ge(*((B["a_loaded"][0], 16 * (IT + 2)) if tail else this(B["a_loaded"], par, i, 16)))
                dve.wait_ge(*two_ago(B["stored"], par, i, 16))
                dve.wait_ge(*two_ago(B["act_normed"], par, i))
                for c, q in pieces(tail):
                    n = c.stop - c.start
                    deg = rdeg[0:q, bass.ds(r * CHUNKS + c.start, n)].unsqueeze(2).broadcast_to([q, n, D])
                    ins = nc.vector.tensor_tensor(res[0:q, par, c, :], aux[0:q, par, c, :], deg, ALU.mult)
                link_(ins)
                for c, q in pieces(tail):
                    y = xin[0:q, par, c, :] if spill else kept(i, par)[0:q, c, :]
                    ins = nc.vector.tensor_tensor(res[0:q, par, c, :], res[0:q, par, c, :], y, ALU.add)
                ins.then_inc(B["added"][par], 1)
                dve.wait_ge(*this(B["added"], par, i))
                for c, q in chunk_parts(tail):
                    ins = nc.vector.bn_stats(st6[0:q, par, ROWS + c, :], res[0:q, par, c, :])
                link_(ins)
                nc.vector.tensor_copy(cols[:, par, 0:2, :], src_tab[:, r, :, :])
                for c, q in chunk_parts(tail):
                    ins = nc.vector.bn_aggr(mv[0:q, par, ROWS + c, :], st6[0:q, par, ROWS + c, :])
                ins.then_inc(B["mv_ready"][par], 1)
                compare(B, i, par, tail)
                scales(B, i, par)

            sweep(dve, chained(body_b, 6), (KEPT,))
            done[0] += (RF + 1) * 6

            def count_batch(ph, i, par, tail, stretch):
                dve.wait_ge(*this(ph["silu"], par, i))
                for n in range(2):
                    p = NODE_TAIL[n] if tail else P
                    c = slice(n * ROWS, (n + 1) * ROWS)
                    ins = nc.vector.bn_stats(bst[:, bass.ds((2 * i + par) * 2 + n, 1), :].rearrange("p a s -> p (a s)"),
                                             z_later(i, par)[:, c, 0:p])
                ins.then_inc(ph["stats"][par], 1)

            def body_c(before, now, after):
                i, par, tail, stretch = now
                dve.wait_ge(*this(C["transposed"], par, i))
                if stretch == 1:
                    dve.wait_ge(s_fetched, 16 * (2 * (i - KEPT) + par + 1))
                if stretch == 2:
                    dve.wait_ge(*late(i, par, tail, 1))
                for c, p in pieces(tail):
                    t = z_later(i, par)[:, c, 0:p]
                    ins = nc.vector.tensor_tensor(t, ps2[par][:, c, 0:p], t, ALU.add)
                ins.then_inc(C["added"][par], 1)
                if before:
                    count_batch(C, *before)

            sweep(dve, body_c, (KEPT, KEPT_LATER))
            count_batch(C, IT, 0, True, 2)

            def fold(k, sems):
                dve.wait_ge(*this(sems, 1, IT - 1))
                dve.wait_ge(*this(sems, 0, IT))
                nc.vector.bn_aggr(bn[:, k, 0:2], bst[:, :, :].rearrange("p a s -> p (a s)")).then_inc(s_bn[k], 1)
                dve.wait_ge(s_bn[k], 2)
                nc.vector.reciprocal(bn[:, k, 3:4], bn[:, k, 2:3]).then_inc(s_bn[k], 1)
                dve.wait_ge(s_bn[k], 3)
                nc.vector.tensor_tensor(bn[:, k, 4:5], bn[:, k, 3:4], vecs[:, 3 * k + 1:3 * k + 2], ALU.mult)\
                    .then_inc(s_bn[k], 1)
                dve.wait_ge(s_bn[k], 4)
                nc.vector.tensor_tensor(bn[:, k, 5:6], bn[:, k, 4:5], bn[:, k, 0:1], ALU.mult).then_inc(s_bn[k], 1)
                dve.wait_ge(s_bn[k], 5)
                nc.vector.tensor_tensor(bn[:, k, 6:7], vecs[:, 3 * k + 2:3 * k + 3], bn[:, k, 5:6], ALU.subtract)\
                    .then_inc(s_bn[k], 1)

            dve.wait_ge(s_w, 16 * 13)
            fold(0, C["stats"])
            nc.vector.tensor_scalar(w2s[:, :], w2[:, :], bn[:, 0, 4:5], None, ALU.mult).then_inc(s_bn[0], 1)
            dve.wait_ge(s_bw, 1)
            nc.vector.tensor_tensor(bn[:, 0, 7:8], psB[:, 0:1], vecs[:, 3:4], ALU.add).then_inc(s_bn[0], 1)

            def body_f(before, now, after):
                count_batch(F, *now)

            sweep(dve, body_f, (KEPT_LATER,))
            fold(1, F["stats"])

            def finish(i, half, odd, par, tail=False):
                dve.wait_ge(x1_loaded[odd][par], 16 * (half + (2 if tail else 1)))
                chain["at"], chain["n"] = done[0] + 2 * i + par, 0
                t = x1_place(i, par)
                for c, q in pieces(tail):
                    b3c = b3b[0:q, :].unsqueeze(1).broadcast_to([q, c.stop - c.start, D])
                    ins = nc.vector.tensor_tensor(t[0:q, c, :], t[0:q, c, :], b3c, ALU.add)
                link_(ins)
                dve.wait_ge(*this(G["product"], par, i))
                for c, q in pieces(tail):
                    ins = nc.vector.tensor_tensor(t[0:q, c, :], t[0:q, c, :], ps2[par][0:q, c, :], ALU.add)
                ins.then_inc(G["done"][par], 1)

            for i in range(3):
                for par in range(2):
                    finish(i, i // 2, i % 2, par)
            doubled(dve, finish, 3, IT - 1)
            for i, par, tail in late_rounds()[4:]:
                finish(i, i // 2, i % 2, par, tail)

        @block.tensor
        def _(pe):
            pe.wait_ge(s_const, 5)
            pe.wait_ge(s_w, 16 * 13)
            pe.wait_ge(s_z0, 1)
            nc.tensor.matmul(psH, hotp[:, 0, 0, :], hotc[:, 0, 0, :], start=True, stop=False).then_inc(s_z0, 1)

            def count_edges(i, par, tail):
                p = edge_parts(tail)
                pe.wait_ge(*this(H["ready"], par, i))
                for j in range(ROWS):
                    ins = nc.tensor.matmul(psH, hotp[0:p, par, j, :], hotc[0:p, par, j, :], start=False,
                                           stop=bool(tail and j == ROWS - 1))
                ins.then_inc(H["used"][par], 1)

            rounds(pe, count_edges)
            count_edges(IT, 0, True)

            def transposes(t, ps_t, tail):
                for c, p in chunk_parts(tail):
                    ins = nc.tensor.transpose(ps_t[:, c, 0:p], t[0:p, c, :], ident[0:p, 0:p])
                return ins

            def presum(t, par, tail):
                p = edge_parts(tail)
                for j in reversed(range(ROWS)):
                    at = j * (j + 1) // 2
                    ins = nc.tensor.matmul(psA[:, 0:j + 1, 0:p], t[0:p, par, j, :], same[0:p, par, at:at + j + 1, 0:p],
                                           start=(j == ROWS - 1), stop=(j == 0))
                return ins

            def edge_product(w, par, tail):
                p = edge_parts(tail)
                for j in range(ROWS):
                    ins = nc.tensor.matmul(psV[0:p, j, :], sumT[:, j, 0:p], w[:, :], start=True, stop=True)
                return ins

            def round_a(i, par, tail):
                pe.wait_ge(*this(A["h_ready"], par, i))
                pe.wait_ge(*this(A["targets"], par, i))
                pe.wait_ge(*last(A["sum_copied"], par, i))
                presum(hE, par, tail).then_inc(A["summed"][par], 1)
                pe.wait_ge(*this(A["normed"], par, i))
                pe.wait_ge(*this(A["act_normed"], par, i))
                pe.wait_ge(*last(A["relu"], par, i))
                transposes(aux[:, par, :, :], psR, tail).then_inc(A["transposed"][par], 1)
                pe.wait_ge(*this(A["sum_copied"], par, i))
                pe.wait_ge(*last(A["v_copied"], par, i))
                edge_product(wl, par, tail).then_inc(A["v_ready"][par], 1)
                pe.wait_ge(*this(A["relu"], par, i))
                pe.wait_ge(*last(A["added"], par, i))
                for c, q in chunk_parts(tail):
                    ins = nc.tensor.matmul(psQ[0:q, c, :], hT[:, par, c, 0:q], wr[:, :], start=True, stop=True)
                ins.then_inc(A["product"][par], 1)

            rounds(pe, round_a)
            round_a(IT, 0, True)

            def round_b(i, par, tail):
                pe.wait_ge(*this(B["rows_loaded"], par, i, 16))
                pe.wait_ge(*this(B["targets"], par, i))
                pe.wait_ge(*last(B["sum_copied"], par, i))
                presum(rows, par, tail).then_inc(B["summed"][par], 1)
                pe.wait_ge(*this(B["act_normed"], par, i))
                pe.wait_ge(*last(B["relu"], par, i))
                transposes(normed_b, psR, tail).then_inc(B["transposed"][par], 1)
                pe.wait_ge(*this(B["sum_copied"], par, i))
                pe.wait_ge(*last(B["v_copied"], par, i))
                edge_product(w1b, par, tail).then_inc(B["v_ready"][par], 1)
                pe.wait_ge(*this(B["relu"], par, i))
                pe.wait_ge(*last(B["z_copied"], par, i))
                for n in range(2):
                    q = NODE_TAIL[n] if tail else P
                    c = slice(n * ROWS, (n + 1) * ROWS)
                    ins = nc.tensor.matmul(psQ[:, c, 0:q], w1a[:, :], hT[:, par, c, 0:q], start=True, stop=True)
                ins.then_inc(B["product"][par], 1)

            rounds(pe, round_b)
            round_b(IT, 0, True)

            def round_c(i, half, odd, par, tail=False):
                pe.wait_ge(acc2_loaded[odd][par], 16 * (half + (2 if tail else 1)))
                pe.wait_ge(*two_ago(C["added"], par, i))
                transposes(acc2_pair(i, odd)[:, par, :, :], ps2[par], tail).then_inc(C["transposed"][par], 1)

            pe.wait_ge(*this(B["relu"], 0, IT))
            pe.wait_ge(*this(B["z_copied"], 0, IT))
            for i in range(3):
                for par in range(2):
                    round_c(i, i // 2, i % 2, par)
            doubled(pe, round_c, 3, KEPT_LATER)
            for i, par, tail in late_rounds():
                round_c(i, i // 2, i % 2, par, tail)

            pe.wait_ge(s_bn[0], 7)
            nc.tensor.matmul(psB[:, 0:1], w2[:, :], bn[:, 0, 6:7], start=True, stop=True).then_inc(s_bw, 1)

            def round_f(i, par, tail):
                pe.wait_ge(*two_ago(F["silu"], par, i))
                if type(i) is int and i >= KEPT_LATER:
                    pe.wait_ge(*late(i, par, tail, 2))
                for n in range(2):
                    q = NODE_TAIL[n] if tail else P
                    c = slice(n * ROWS, (n + 1) * ROWS)
                    ins = nc.tensor.matmul(ps2[par][:, c, 0:q], w2s[:, :], z_later(i, par)[:, c, 0:q],
                                           start=True, stop=True)
                ins.then_inc(F["product"][par], 1)

            rounds(pe, round_f, 0, KEPT_LATER)
            for r in late_rounds():
                round_f(*r)

            def round_g(i, par, tail):
                pe.wait_ge(*this(G["scaled"], par, i))
                pe.wait_ge(*two_ago(G["done"], par, i))
                for c, q in chunk_parts(tail):
                    ins = nc.tensor.matmul(ps2[par][0:q, c, :], hT[:, par, c, 0:q], w3[:, :], start=True, stop=True)
                ins.then_inc(G["product"][par], 1)

            pe.wait_ge(*this(F["silu"], 0, IT))
            pe.wait_ge(*this(F["silu"], 1, IT - 1))
            rounds(pe, round_g)
            round_g(IT, 0, True)


_ARGS = ["x", "src", "dst", "edge_attr_128", "L0_gnn_W_l", "L0_gnn_W_r", "L1_gnn_W1", "L1_gnn_b1", "L1_gnn_g1",
         "L1_gnn_be1", "L1_gnn_W2", "L1_gnn_b2", "L1_gnn_g2", "L1_gnn_be2", "L1_gnn_W3", "L1_gnn_b3"]


def kernel(**inputs):
    import numpy as _np
    import concourse.bacc as _bacc
    from concourse import mybir as _mybir
    from concourse.bass_utils import run_bass_kernel_spmd as _run

    nc = _bacc.Bacc("TRN2", target_bir_lowering=False, num_devices=1)
    arrays, args = {}, []
    for name in _ARGS:
        a = _np.asarray(inputs[name])
        if name in ("L0_gnn_W_l", "L0_gnn_W_r"):
            a = a.T
        a = _np.ascontiguousarray(a)
        arrays[f"in_{name}_dram"] = a
        args.append(nc.dram_tensor(f"in_{name}_dram", a.shape, _mybir.dt.from_np(a.dtype), kind="ExternalInput").ap())
    shape = tuple(inputs["x"].shape)
    args.append(nc.dram_tensor("out_0_dram", shape, _mybir.dt.float32, kind="ExternalOutput").ap())
    gnn_layers(nc, *args)
    r = _run(nc, [arrays], core_ids=[0])
    return r.results[0]["out_0_dram"]
```

```python
from contextlib import ExitStack

import concourse.bass as bass
from concourse import mybir

P = 128
ROWS = 4
GROUP = P * ROWS
CHUNKS = 2 * ROWS
ROUND = 2 * GROUP


def this(sem, par, i, inc=1):
    return sem[par], (i + 1) * inc


def two_ago(sem, par, i, inc=1):
    return sem[par], i * inc


def last(sem, par, i, inc=1):
    return sem[1 - par], (i + par) * inc


def gnn_layers(nc, x, src, dst, edge_attr, WlT, WrT, W1, b1, g1, be1, W2, b2, g2, be2, W3, b3, out):
    fp32 = mybir.dt.float32
    fp16 = mybir.dt.float16
    i32 = mybir.dt.int32
    u32 = mybir.dt.uint32
    ALU = mybir.AluOpType
    ACT = mybir.ActivationFunctionType

    N, D = x.shape
    E = src.shape[0]
    EPS = 1e-5
    STEPS = 2
    ACT_H = 2
    ACT_A = 6

    RF = N // ROUND
    IT = RF // 2
    NODE_TAIL = [P, (N - RF * ROUND - GROUP) // ROWS]
    EDGE_TAIL = (E - RF * GROUP) // ROWS
    assert RF % 2 == 0 and E // GROUP == RF and GROUP + NODE_TAIL[1] * ROWS == N - RF * ROUND
    assert EDGE_TAIL * ROWS == E - RF * GROUP and 0 < EDGE_TAIL <= P and 0 < NODE_TAIL[1] <= P
    KEPT = 16
    KEPT_LATER = 21
    SPILLED = IT - KEPT
    assert 3 <= SPILLED <= KEPT < KEPT_LATER == IT - 3 and KEPT_LATER % 2 == 1
    EARLY_G = 7
    MID_F = 13
    MID_C = 11
    DVE_C = 5
    assert ROWS <= DVE_C < CHUNKS
    PRE = 14
    assert SPILLED < PRE < IT - 3 and all(4 * (i - SPILLED) + 3 - (4 * SPILLED - PRE) <= i - 2
                                          for i in range(SPILLED, 2 * SPILLED))
    FETCHED = 2 * (KEPT_LATER - KEPT)
    assert FETCHED == 10
    ACC_ROWS = 3 * P * -(-(N + GROUP) // (3 * P))
    ZPARTS = 12
    ZREP = 2
    ZCOLS = ACC_ROWS * D // P // RF // ZREP
    assert ZCOLS * RF * ZREP * P == ACC_ROWS * D and RF == 4 * ZPARTS
    COLS = (RF + 1) * CHUNKS

    def node_rows(t):
        full = t[0:RF * ROUND, :].rearrange("(r n p j) d -> r p n (j d)", n=2, p=P, j=ROWS)
        a = t[RF * ROUND:RF * ROUND + GROUP, :].rearrange("(p j) d -> p (j d)", j=ROWS)
        b = t[RF * ROUND + GROUP:N, :].rearrange("(p j) d -> p (j d)", j=ROWS)
        return full, (a, b)

    def edge_cols(t):
        return (t[0:RF * GROUP].rearrange("(r p j) -> r p j", p=P, j=ROWS),
                t[RF * GROUP:E].rearrange("(p j) -> p j", j=ROWS))

    acc1 = nc.dram_tensor("acc1", (ACC_ROWS, D), fp32).ap()
    acc2 = nc.dram_tensor("acc2", (ACC_ROWS, D), fp32).ap()
    y_dram = nc.dram_tensor("y_dram", (N, D), fp32).ap()
    x1_dram = nc.dram_tensor("x1_dram", (N, D), fp32).ap()
    z_dram = nc.dram_tensor("z_dram", (RF - 2 * KEPT + 1, P, ROUND), fp32).ap()
    zz_dram = nc.dram_tensor("zz_dram", (RF - 2 * KEPT_LATER + 1, P, ROUND), fp32).ap()
    zy_dram = nc.dram_tensor("zy_dram", (RF - 2 * KEPT_LATER + 1, P, ROUND), fp32).ap()

    x_v, y_v, x1_v, out_v = (node_rows(t) for t in (x, y_dram, x1_dram, out))
    acc1_v, acc2_v = node_rows(acc1[0:N, :]), node_rows(acc2[0:N, :])
    src_v, dst_v = edge_cols(src), edge_cols(dst)
    src_row = src[0:RF * GROUP].rearrange("(r k) -> r k", k=GROUP)
    dst_row = dst[0:RF * GROUP].rearrange("(r k) -> r k", k=GROUP)
    ea_v = (edge_attr[0:RF * GROUP, :].rearrange("(r p j) d -> r p (j d)", p=P, j=ROWS),
            edge_attr[RF * GROUP:E, :].rearrange("(p j) d -> p (j d)", j=ROWS))
    acc1_z = acc1.rearrange("(p r) d -> p (r d)", p=P).rearrange("p (k a c) -> k p a c", k=ZPARTS, c=ZCOLS)
    acc2_z = acc2.rearrange("(p r) d -> p (r d)", p=P).rearrange("p (k a c) -> k p a c", k=RF, c=ZCOLS)

    def column(t):
        return t.rearrange("(p a) -> p a", a=1)

    ctx = ExitStack()
    with ctx:
        def sb(name, shape, dt=fp32):
            return ctx.enter_context(nc.sbuf_tensor(name, shape, dt))

        def sem(name):
            return ctx.enter_context(nc.semaphore(name))

        def pair(name):
            return [sem(f"{name}_{k}") for k in range(2)]

        wl = sb("wl", [P, D]); wr = sb("wr", [P, D]); w1a = sb("w1a", [P, D]); w1b = sb("w1b", [P, D])
        w2 = sb("w2", [P, D]); w3 = sb("w3", [P, D]); w2s = sb("w2s", [P, D])
        b3b = sb("b3b", [P, D])
        vecs = sb("vecs", [P, 6])
        ident = sb("ident", [P, P])
        eps = sb("eps", [P, 1])
        iota_p = sb("iota_p", [P, P], fp16)
        warm = sb("warm", [P, 1])
        zeros = sb("zeros", [P, ZCOLS])
        dump = sb("dump", [P, ROWS])
        dst_tab = sb("dst_tab", [P, RF + 1, 4, ROWS])
        src_tab = sb("src_tab", [P, RF + 1, 2, ROWS])
        rdeg = sb("rdeg", [P, COLS])
        xin = sb("xin", [P, 2, CHUNKS, D])
        zT = sb("zT", [P, 2 * KEPT_LATER, ROUND])
        zflat = zT[:, :, :].rearrange("p r c -> p (r c)")
        taken = [2 * KEPT * ROUND]

        def part(shape, dt=fp32):
            n = 1
            for k in shape[1:]:
                n *= k
            at = taken[0]
            taken[0] += n
            assert taken[0] <= 2 * KEPT_LATER * ROUND
            t = zflat[:, at:at + n]
            if dt is not fp32:
                t = t.bitcast(dt)
            names = "abcd"[:len(shape) - 1]
            sizes = dict(zip(names, shape[1:]))
            return t.rearrange(f"p ({' '.join(names)}) -> p {' '.join(names)}", **sizes)

        order = part([P, ROWS, P])
        icol_pre = zflat[:, 0:PRE * ROWS].bitcast(u32).rearrange("p (r j) -> p r j", j=ROWS)
        rows_pre = zflat[:, (4 * SPILLED - PRE) * ROWS * D:4 * SPILLED * ROWS * D]\
            .rearrange("p (r j d) -> p r j d", r=PRE, j=ROWS)
        aux = part([P, 2, CHUNKS, D])
        table_ints = aux[:, :, :, :].rearrange("p a c d -> p (a c d)").bitcast(i32)
        IC = (RF + 1) * ROWS
        raw = table_ints[:, 0:2 * IC].rearrange("p (k c) -> p k c", k=2)
        ints = table_ints[:, 2 * IC:4 * IC].rearrange("p (k c) -> p k c", k=2)
        res = sb("res", [P, 2, CHUNKS, D])
        hT = sb("hT", [P, 2, CHUNKS, P])
        rows = part([P, 2, ROWS, D])
        hE = part([P, 2, ROWS, D])
        normed_b = hE[:, :, :, :].rearrange("p a j d -> p (a j) d")
        same = part([P, 2, ROWS * (ROWS + 1) // 2, P])
        hots = same[:, :, :, :].rearrange("p a b c -> p a (b c)").bitcast(fp16)
        hotp = hots[:, :, 0:ROWS * P].rearrange("p a (j c) -> p a j c", j=ROWS)
        hotc = hots[:, :, ROWS * P:ROWS * (P + COLS)].rearrange("p a (j c) -> p a j c", j=ROWS)
        sumT = part([P, ROWS, P])
        vrow = part([P, 2, ROWS, D])
        irow = part([P, 2, GROUP], i32)
        iota_c = part([P, COLS // 2]).bitcast(fp16)
        icol = sb("icol", [P, 2, ROWS], u32)
        cols = part([P, 2, 4, ROWS])
        count = sb("count", [P, 2, ROWS])
        shift = sb("shift", [P, 2, ROWS])
        target = sb("target", [P, 2, ROWS], u32)
        st6 = part([P, 2, 12, 6])
        mv = part([P, 2, 12, 2])
        sd = part([P, 2, 12])
        rs = part([P, 2, 12])
        nm = part([P, 2, 12])
        bst = sb("bst", [P, 2 * (RF + 1), 6])
        bn = sb("bn", [P, 2, 8])

        ps = ctx.enter_context(nc.psum_tensor("ps", [P, 8, 512], fp32))
        psR = ps[:, 0:2, :].rearrange("p b (j c) -> p (b j) c", c=P)
        psQ = ps[:, 2:4, :].rearrange("p b (j c) -> p (b j) c", c=P)
        psA = ps[:, 4, :].rearrange("p (j c) -> p j c", c=P)
        psV = ps[:, 5, :].rearrange("p (j c) -> p j c", c=P)
        psH = ps[:, 6, 0:COLS]
        psB = ps[:, 7, :]
        ps2 = [ps[:, 2 * k:2 * k + 2, :].rearrange("p b (j c) -> p (b j) c", c=P) for k in range(2)]

        ps4 = [[ps[:, 4 * o + 2 * k:4 * o + 2 * k + 2, :].rearrange("p b (j c) -> p (b j) c", c=P) for k in range(2)]
               for o in range(2)]

        s_w = sem("weights_loaded")
        s_idx = sem("indices_loaded")
        s_const = sem("constants_made")
        s_mem = sem("memsets_done")
        s_chain = sem("vector_chain")
        s_zero1 = sem("acc1_zeroed")
        s_zero2 = sem("acc2_zeroed")
        s_turn = sem("pool_turn")

        def phase(tag, names):
            return {k: pair(f"{tag}_{k}") for k in names.split()}

        common = ("row_loaded rows_loaded mv_ready sd_ready act_normed nm_ready compared targets transposed "
                  "relu product summed sum_copied v_ready v_copied added stored")
        A = phase("a", common + " normed x_loaded icol_loaded h_ready")
        H = phase("h", "columns squared ready_p ready_c used")
        s_pre_idx = sem("pre_indices_loaded")
        s_pre = sem("pre_rows_loaded")
        B = phase("b", common + " y_loaded a_loaded z_copied z_stored")
        C = phase("c", "transposed added silu stats stored")
        F = phase("f", "product silu stats stored")
        G = phase("g", "scaled product done stored early_stored")
        acc2_loaded = [pair(f"acc2_loaded_{k}") for k in range(2)]
        x1_loaded = [pair(f"x1_loaded_{k}") for k in range(2)]
        late_loaded = [sem(f"late_loaded_{r}") for r in range(2 * KEPT_LATER, RF + 1)]
        s_sc1 = pair("acc1_scattered")
        s_sc2 = pair("acc2_scattered")
        s_z0 = sem("hist_opened")
        s_set = sem("eps_then_zeros_set")
        s_fetched = sem("z_fetched")
        s_bn = pair("bn_steps")
        s_bw = sem("bn_bias_product")

        block = ctx.enter_context(nc.Block())

        def pieces(tail):
            return [(slice(0, ROWS), NODE_TAIL[0]), (slice(ROWS, CHUNKS), NODE_TAIL[1])] if tail else \
                [(slice(0, CHUNKS), P)]

        def chunk_parts(tail):
            return [(c, NODE_TAIL[c // ROWS] if tail else P) for c in range(CHUNKS)]

        def edge_parts(tail):
            return EDGE_TAIL if tail else P

        def rounds(eng, body, lo=0, hi=IT):
            if hi > lo:
                for par in range(2):
                    body(lo, par, False)
            if hi > lo + 1:
                with eng.Fori(lo + 1, hi) as i:
                    for par in range(2):
                        body(i, par, False)

        def sweep(eng, body, bounds, wide=False, margin=1):
            def fixed(r):
                return (r // 2, r % 2, r == RF, sum(b <= r // 2 for b in bounds)) if 0 <= r <= RF else None

            n = 4 if wide else 3

            def peeled(lo, hi):
                for r in range(lo, hi):
                    body(*(fixed(r + k) for k in range(-1, n - 1)))

            at = 0
            for k, (lo, hi) in enumerate(zip((0, *bounds), (*bounds, IT))):
                top = hi - margin
                first = top - (top - lo - 2) // STEPS * STEPS
                if top > first:
                    peeled(at, 2 * first)
                    with eng.Fori(first, top + 1 - STEPS, STEPS) as i:
                        near = [(i - 1, 1, False, k)]
                        near += [(i + j, par, False, k) for j in range(STEPS + 1) for par in range(2)]
                        for j in range(2 * STEPS):
                            body(*near[j:j + n])
                    at = 2 * top
            peeled(at, RF + 1)

        def doubled(eng, body, lo, hi):
            assert (hi - lo) % 2 == 0
            with eng.Fori(0, (hi - lo) // 2) as k:
                for q in range(2):
                    for par in range(2):
                        body(2 * k + lo + q, k + (lo + q) // 2, (lo + q) % 2, par)

        def split_c(tail):
            if tail:
                return [(slice(0, ROWS), NODE_TAIL[0]), (slice(ROWS, DVE_C), NODE_TAIL[1])], \
                    (slice(DVE_C, CHUNKS), NODE_TAIL[1])
            return [(slice(0, DVE_C), P)], (slice(DVE_C, CHUNKS), P)

        def late_rounds():
            return [(r // 2, r % 2, r == RF) for r in range(2 * KEPT_LATER, RF + 1)]

        def late(i, par, tail, times):
            return late_loaded[2 * (i - KEPT_LATER) + par], 32 * (times + 1) if tail else 16 * times

        def iteration_c(n):
            return n if n < 3 or n == IT else \
                {3: KEPT_LATER, MID_C: IT - 1, IT - 1: IT - 2}.get(n, n - 1 if n < MID_C else n - 2)

        def iteration_f(n, shift):
            if type(n) is not int:
                return n - shift
            return n if n < 3 or n == IT else {3: KEPT_LATER, 4: KEPT_LATER + 1, MID_F: IT - 1}.get(n, n - shift)

        def walk_c(eng, body):
            def fixed(lo, hi, fetched):
                for n in range(lo, hi):
                    for par in range(2):
                        body(n, iteration_c(n), n // 2, n % 2, par, False, fetched)

            def loop(lo, hi, shift, fetched):
                doubled(eng, lambda n, half, odd, par: body(n, n - shift, half, odd, par, False, fetched), lo, hi)

            fixed(0, 5, False)
            loop(5, MID_C, 1, False)
            fixed(MID_C, MID_C + 2, False)
            loop(MID_C + 2, KEPT + 1, 2, False)
            fixed(KEPT + 1, KEPT + 2, False)
            fixed(KEPT + 2, KEPT + 3, True)
            loop(KEPT + 3, IT - 1, 2, True)
            fixed(IT - 1, IT, False)
            body(IT, IT, IT // 2, IT % 2, 0, True, False)

        def walk_f(eng, body):
            def fixed(lo, hi, shift):
                for n in range(lo, hi):
                    for par in range(2):
                        body(n, iteration_f(n, shift), par, False)

            def loop(lo, hi, shift):
                with eng.Fori(lo, hi) as n:
                    for par in range(2):
                        body(n, n - shift, par, False)

            fixed(0, 5, 2)
            loop(5, MID_F, 2)
            fixed(MID_F, MID_F + 1, 3)
            loop(MID_F + 1, IT, 3)
            body(IT, IT, 0, True)

        def returned(i, par, tail, fetched):
            if fetched:
                return s_fetched, 16 * (2 * (i - KEPT) + par + 1)
            return late(i, par, tail, 1) if type(i) is int and i >= KEPT_LATER else None

        def acc2_place(n, odd, par):
            return hT[:, 1, :, :] if type(n) is int and n == IT else (xin if odd else res)[:, par, :, :]

        def z_later(i, par):
            if type(i) is int and i >= KEPT_LATER:
                return (hT if i % 2 else res)[:, par, :, :]
            return kept(i, par)

        def z_third(i, par):
            return hT[:, par, :, :] if type(i) is int and i == IT else z_later(i, par)

        def x1_place(i, par):
            if type(i) is int and not 2 <= i < IT - 1:
                return (xin if i in (0, IT - 1) else res)[:, par, :, :]
            return kept(i - 2, par)

        def kept(i, par):
            return zT[:, 2 * i + par, :].rearrange("p (c q) -> p c q", q=P)

        def place_a(i, par, late):
            return (2 * (i - SPILLED) + par, kept(i - SPILLED, par)) if late else \
                (2 * (i + KEPT) + par, kept(i + KEPT - SPILLED, par))

        def two_back(i, par, tail, stretch):
            if type(i) is not int:
                return i - 1, par, False, stretch
            return (i - 1, par, False, (SPILLED < i) + (PRE < i)) if i else None

        def gathered(i, par, stretch):
            return par == 0 or stretch == 2

        def edge_rows(i, par, stretch):
            return rows[:, par, :, :] if gathered(i, par, stretch) else rows_pre[:, i, :, :]

        def gathers(sem, par, i, inc):
            return sem[par], (i - PRE if par else i) * inc

        def round_a_of(i, par, tail, late):
            return RF if tail else place_a(i, par, late)[0]

        def rows_a(i, par, tail, late):
            return xin[:, par, :, :] if tail else place_a(i, par, late)[1]

        def spilled(d, t, tail):
            if not tail:
                return [(d, t.rearrange("p c q -> p (c q)"))]
            d = d.rearrange("f (c q) -> f c q", q=P)
            return [(d[:, c, 0:p], t[:, c, 0:p]) for c, p in pieces(True)]

        @block.sync
        def _(sp):
            sp.wait_ge(s_mem, 1)
            for k, v in enumerate((dst_v, src_v)):
                sp.dma_start(raw[:, k, 0:RF * ROWS].rearrange("p (r j) -> p r j", j=ROWS),
                             v[0].rearrange("r p j -> p r j")).then_inc(s_idx, 16)
                sp.dma_start(raw[0:EDGE_TAIL, k, RF * ROWS:], v[1]).then_inc(s_idx, 16)
            for t, w in ((wl, WlT), (wr, WrT), (w1a, W1[0:D, :]), (w1b, W1[D:2 * D, :]), (w2, W2), (w3, W3)):
                sp.dma_start(t[:, :], w).then_inc(s_w, 16)
            for k, v in enumerate((b1, g1, be1, b2, g2, be2)):
                sp.dma_start(vecs[:, k:k + 1], column(v)).then_inc(s_w, 16)
            sp.dma_start(b3b[:, :], b3.partition_broadcast(P)).then_inc(s_w, 16)

            def load_nodes(t, v, r, tail, sem):
                for n in range(2 if tail else 0):
                    p = NODE_TAIL[n]
                    sp.dma_start(t[0:p, n * ROWS:(n + 1) * ROWS, :].rearrange("p j d -> p (j d)"),
                                 v[1][n]).then_inc(sem, 16)
                if not tail:
                    sp.dma_start(t.rearrange("p (n j) d -> p n (j d)", n=2), v[0][r]).then_inc(sem, 16)

            def store_nodes(t, v, r, tail, sem):
                for n in range(2 if tail else 0):
                    p = NODE_TAIL[n]
                    sp.dma_start(v[1][n], t[0:p, n * ROWS:(n + 1) * ROWS, :].rearrange("p j d -> p (j d)"))\
                        .then_inc(sem, 16)
                if not tail:
                    sp.dma_start(v[0][r], t.rearrange("p (n j) d -> p n (j d)", n=2)).then_inc(sem, 16)

            def load_a(i, par, tail, late):
                r = round_a_of(i, par, tail, late)
                if gathered(i, par, late):
                    sp.wait_ge(*gathers(A["rows_loaded"], par, i, 64))
                dst_i, src_i = (dst[RF * GROUP:E], src_v[1]) if tail else (dst_row[r], src_v[0][r])
                p = EDGE_TAIL if tail else P
                if gathered(i, par, late):
                    sp.dma_start(icol[0:p, par, :], src_i.bitcast(u32)).then_inc(A["icol_loaded"][par], 16)
                sp.wait_ge(*two_ago(A["compared"], par, i))
                sp.dma_start(irow[:, par, 0:p * ROWS], dst_i.partition_broadcast(P))\
                    .then_inc(A["row_loaded"][par], 16)
                if late:
                    sp.wait_ge(A["h_ready"][1], i - 1)
                sp.wait_ge(*two_ago(A["mv_ready"], par, i))
                load_nodes(rows_a(i, par, tail, late), x_v, r, tail, A["x_loaded"][par])

            def store_a(i, par, tail, late):
                if not tail:
                    sp.dma_start(acc2_z[2 * i + par], zeros[:, :].unsqueeze(1).broadcast_to([P, ZREP, ZCOLS]))\
                        .then_inc(s_zero2, 16)
                if tail or not late:
                    sp.wait_ge(*this(A["added"], par, i))
                    store_nodes(res[:, par, :, :] if tail else rows_a(i, par, tail, late), y_v,
                                round_a_of(i, par, tail, late), tail, A["stored"][par])
                else:
                    sp.wait_ge(A["stored"][par], 16 * SPILLED)

            def step_a(before, now, after, ahead):
                if ahead:
                    load_a(*ahead)
                if two_back(*now):
                    store_a(*two_back(*now))

            def all_stored(sems, kept_its):
                sp.wait_ge(sems[0], 16 * (IT - kept_its + 2))
                sp.wait_ge(sems[1], 16 * (IT - kept_its))

            def clear_acc1():
                sp.wait_ge(s_set, 2)
                for k in range(ZPARTS):
                    sp.dma_start(acc1_z[k], zeros[:, :].unsqueeze(1).broadcast_to([P, 4 * ZREP, ZCOLS]))\
                        .then_inc(s_zero1, 16)

            load_a(0, 0, False, False)
            sp.dma_start(icol_pre[:, 0:SPILLED, :],
                         src_v[0][2 * KEPT + 1:RF:2].rearrange("r p j -> p r j").bitcast(u32)).then_inc(s_pre_idx, 16)
            sp.dma_start(icol_pre[:, SPILLED:PRE, :],
                         src_v[0][1:2 * (PRE - SPILLED):2].rearrange("r p j -> p r j").bitcast(u32))\
                .then_inc(s_pre_idx, 16)
            load_a(0, 1, False, False)
            clear_acc1()
            sweep(sp, step_a, (SPILLED, PRE), wide=True)
            def load_b_nodes(i, par, tail, spill):
                r = 2 * i + par
                sp.wait_ge(*two_ago(B["added"], par, i))
                load_nodes(aux[:, par, :, :], acc1_v, r, tail, B["a_loaded"][par])
                if spill:
                    load_nodes(xin[:, par, :, :], y_v, r, tail, B["y_loaded"][par])

            def load_b_edges(i, par, tail, spill):
                r = 2 * i + par
                src_i, ea = (src[RF * GROUP:E], ea_v[1]) if tail else (src_row[r], ea_v[0][r])
                p = EDGE_TAIL if tail else P
                sp.wait_ge(*two_ago(B["compared"], par, i))
                sp.dma_start(irow[:, par, 0:p * ROWS], src_i.partition_broadcast(P))\
                    .then_inc(B["row_loaded"][par], 16)
                sp.wait_ge(*two_ago(B["summed"], par, i))
                sp.dma_start(rows[0:p, par, :, :].rearrange("p j d -> p (j d)"), ea)\
                    .then_inc(B["rows_loaded"][par], 16)

            sp.wait_ge(*this(A["compared"], 0, IT))
            sp.wait_ge(*this(A["compared"], 1, IT - 1))
            sp.wait_ge(*this(A["h_ready"], 0, IT))
            sp.wait_ge(*this(A["h_ready"], 1, IT - 1))
            for par in range(2):
                load_b_edges(0, par, False, 0)
            store_a(IT - 1, 1, False, 2)
            store_a(IT, 0, True, 2)

            def step_b(before, now, after, ahead):
                i, par, tail, spill = now
                if ahead:
                    load_b_nodes(*ahead)
                sp.wait_ge(*this(B["added"], par, i))
                store_nodes(res[:, par, :, :], x1_v, 2 * i + par, tail, B["stored"][par])
                if type(i) is not int or 2 * (i + 2) + par <= RF:
                    load_b_edges(i + 2, par, type(i) is int and i + 2 == IT, 0)

            all_stored(A["stored"], KEPT)
            sp.wait_ge(*this(s_sc1, 0, IT, 64))
            sp.wait_ge(*this(s_sc1, 1, IT - 1, 64))
            sp.wait_ge(*this(A["transposed"], 0, IT))
            for par in range(2):
                load_b_nodes(0, par, False, 0)
            for par in range(2):
                load_b_edges(1, par, False, 0)
            sweep(sp, step_b, (KEPT,), wide=True, margin=2)

            sp.wait_ge(*this(s_sc2, 0, IT, 64))
            sp.wait_ge(*this(s_sc2, 1, IT - 1, 64))
            sp.wait_ge(*this(B["stored"], 1, IT - 1, 16))
            sp.wait_ge(B["stored"][0], 16 * (IT + 2))
            sp.wait_ge(*this(B["act_normed"], 0, IT))
            sp.wait_ge(*this(B["act_normed"], 1, IT - 1))

            def load_c(n, i, odd, par, tail=False):
                load_nodes(acc2_place(n, odd, par), acc2_v, 2 * i + par, tail,
                           late_loaded[-1] if tail else acc2_loaded[odd][par])

            def reload_c(n, i, odd, par):
                sp.wait_ge(C["transposed"][par], n - 1)
                load_c(n, i, odd, par)

            def reload_fixed(lo, hi):
                for n in range(lo, hi):
                    for par in range(2):
                        reload_c(n, iteration_c(n), n % 2, par)

            def reload_loop(lo, hi, shift):
                doubled(sp, lambda n, half, odd, par: reload_c(n, n - shift, odd, par), lo, hi)

            def load_late(d, first, i, par, tail, t):
                for a, b in spilled(d[2 * (i - first) + par], t, tail):
                    sp.dma_start(b, a).then_inc(late_loaded[2 * (i - KEPT_LATER) + par], 16)

            def store_z(ph, d, n, i, par, tail=False, place=z_later):
                sp.wait_ge(*this(ph["silu"], par, n))
                sp.wait_ge(*this(ph["stats"], par, n))
                for a, b in spilled(d[2 * (i - KEPT_LATER) + par], place(i, par), tail):
                    sp.dma_start(a, b).then_inc(ph["stored"][par], 16)

            def fetch(k):
                if type(k) is not int or k:
                    sp.wait_ge(s_fetched, 16 * k)
                sp.dma_start(zT[:, 2 * KEPT + k, :], z_dram[k]).then_inc(s_fetched, 16)

            def pre_activations(i, par, tail=False):
                load_late(z_dram, KEPT, i, par, tail, z_third(i, par))

            for n in range(2):
                for par in range(2):
                    load_c(n, n, n, par)
            reload_fixed(2, 3)
            all_stored(B["z_stored"], KEPT)
            for par in range(2):
                pre_activations(KEPT_LATER, par)
            reload_fixed(3, 5)
            fetch(0)
            reload_loop(5, 7, 1)
            for par in range(2):
                store_z(C, zz_dram, 3, KEPT_LATER, par)
            fetch(1)
            reload_loop(7, 9, 1)
            for par in range(2):
                sp.wait_ge(C["stored"][par], 16)
                pre_activations(IT - 1, par)
            fetch(2)
            reload_loop(9, MID_C, 1)
            fetch(3)
            reload_fixed(MID_C, MID_C + 1)
            fetch(4)
            reload_fixed(MID_C + 1, MID_C + 2)
            fetch(5)
            reload_loop(MID_C + 2, MID_C + 4, 2)
            for par in range(2):
                store_z(C, zz_dram, MID_C, IT - 1, par)
            fetch(6)
            reload_loop(MID_C + 4, KEPT + 1, 2)
            fetch(7)
            reload_fixed(KEPT + 1, KEPT + 2)
            sp.wait_ge(C["stored"][0], 32)
            sp.wait_ge(C["stored"][1], 32)
            pre_activations(IT, 0, True)
            load_c(IT, IT, 0, 0, True)
            fetch(8)
            reload_fixed(KEPT + 2, KEPT + 3)
            fetch(9)
            reload_loop(KEPT + 3, IT - 1, 2)
            reload_fixed(IT - 1, IT)
            for par in range(2):
                sp.wait_ge(C["transposed"][par], IT - 1)
                pre_activations(IT - 2, par)
            for par in range(2):
                store_z(C, zz_dram, IT - 1, IT - 2, par)
            store_z(C, zz_dram, IT, IT, 0, True, place=z_third)

            def activations(i, par, tail=False):
                load_late(zz_dram, KEPT_LATER, i, par, tail, z_later(i, par))

            all_stored(C["stored"], KEPT_LATER)
            for i in range(KEPT_LATER, KEPT_LATER + 2):
                for par in range(2):
                    activations(i, par)

            def load_x1(i, odd, par, tail=False):
                load_nodes(x1_place(i, par), x1_v, 2 * i + par, tail, x1_loaded[odd][par])

            for par in range(2):
                load_x1(0, 0, par)
            for par in range(2):
                store_z(F, zy_dram, 3, KEPT_LATER, par)
            for par in range(2):
                sp.wait_ge(F["stored"][par], 16)
                activations(KEPT_LATER + 2, par)
                store_z(F, zy_dram, 4, KEPT_LATER + 1, par)
            sp.wait_ge(F["stored"][0], 32)
            activations(IT, 0, True)
            for par in range(2):
                store_z(F, zy_dram, MID_F, IT - 1, par)
            sp.wait_ge(F["stored"][0], 48)
            store_z(F, zy_dram, IT, IT, 0, True)

            all_stored(F["stored"], KEPT_LATER)
            for par in range(2):
                load_x1(1, 1, par)

            def store_out(i, par, tail=False, early=False):
                sp.wait_ge(*this(G["done"], par, i))
                store_nodes(x1_place(i, par), out_v, 2 * i + par, tail, G["early_stored" if early else "stored"][par])

            def step_g(i, half, odd, par, early=False):
                sp.wait_ge(*this(G["scaled"], par, i))
                sp.wait_ge(x1_loaded[odd][par], 16 * (half + 1))
                load_x1(i + 2, odd, par)
                store_out(i, par, early=early)

            for i in range(3):
                for par in range(2):
                    step_g(i, i // 2, i % 2, par, early=True)
            doubled(sp, lambda *step: step_g(*step, early=True), 3, EARLY_G)
            doubled(sp, step_g, EARLY_G, EARLY_G + 4)
            for par in range(2):
                sp.wait_ge(G["early_stored"][par], 16 * EARLY_G)
            for i, par, tail in late_rounds():
                load_late(zy_dram, KEPT_LATER, i, par, tail, kept(i - KEPT_LATER, par))
            doubled(sp, step_g, EARLY_G + 4, KEPT_LATER)
            for par in range(2):
                sp.wait_ge(x1_loaded[1][par], 16 * (KEPT_LATER // 2 + 1))
                load_x1(IT - 1, 1, par)
                store_out(KEPT_LATER, par)
            sp.wait_ge(x1_loaded[0][0], 16 * (IT // 2))
            load_x1(IT, 0, 0, True)
            for i, par, tail in late_rounds()[2:]:
                store_out(i, par, tail)
            sp.wait_ge(G["stored"][1], 16 * (IT - EARLY_G))
            sp.wait_ge(G["stored"][0], 16 * (IT - EARLY_G + 2))

        @block.gpsimd
        def _(pool):
            nc.gpsimd.memset(raw, 0).then_inc(s_mem, 1)
            nc.gpsimd.memset(ident[:, :], 0.0).then_inc(s_turn, 1)
            nc.gpsimd.memset(order[:, :, :], 1.0).then_inc(s_turn, 1)
            pool.wait_ge(s_turn, 2)
            nc.gpsimd.affine_select(out=ident[:, :], in_=ident[:, :], compare_op=ALU.not_equal, fill=1.0,
                                    base=0, pattern=[[-1, P]], channel_multiplier=1).then_inc(s_const, 1)
            nc.gpsimd.affine_select(out=order[:, ROWS - 1, :], in_=order[:, ROWS - 1, :], compare_op=ALU.is_ge,
                                    fill=0.0, base=0, pattern=[[-1, P]], channel_multiplier=1).then_inc(s_const, 1)
            nc.gpsimd.iota(iota_p[:, :], [[1, P]], base=0, channel_multiplier=0,
                           allow_small_or_imprecise_dtypes=True).then_inc(s_const, 1)
            nc.gpsimd.iota(iota_c[:, :], [[1, COLS]], base=0, channel_multiplier=0,
                           allow_small_or_imprecise_dtypes=True).then_inc(s_const, 1)
            nc.gpsimd.iota(dump[:, :], [[P, ROWS]], base=N, channel_multiplier=1,
                           allow_small_or_imprecise_dtypes=True).then_inc(s_const, 1)

            def hold(s, value):
                pool.wait_ge(s, value)
                pool.sem_inc(s_turn, 1)

            def gather(i, par, tail):
                p = edge_parts(tail)
                hold(*gathers(A["icol_loaded"], par, i + 1, 16))
                hold(*two_ago(A["h_ready"], par, i))
                for j in range(ROWS):
                    pool.indirect_dma_start(
                        rows[0:p, par, j, :], None, x,
                        bass.IndirectOffsetOnAxis(ap=icol[0:p, par, j:j + 1], axis=0))\
                        .then_inc(A["rows_loaded"][par], 16)

            def scatter(ph, acc, s_sc, i, par, tail):
                p = edge_parts(tail)
                hold(*this(ph["v_copied"], par, i))
                hold(*this(ph["targets"], par, i))
                hold(*last(s_sc, par, i, 64))
                for j in range(ROWS):
                    pool.indirect_dma_start(
                        acc, bass.IndirectOffsetOnAxis(ap=target[0:p, par, j:j + 1], axis=0),
                        vrow[0:p, par, j, :], None, compute_op=ALU.add).then_inc(s_sc[par], 16)

            gather(0, 0, False)
            pool.wait_ge(s_pre_idx, 32)
            for g in range(PRE):
                for j in range(ROWS):
                    pool.indirect_dma_start(
                        rows_pre[:, g, j, :], None, x,
                        bass.IndirectOffsetOnAxis(ap=icol_pre[:, g, j:j + 1], axis=0)).then_inc(s_pre, 16)
            pool.wait_ge(s_zero1, 16 * ZPARTS)

            def step_a(i, gather_odd):
                gather(i + 1, 0, False)
                scatter(A, acc1, s_sc1, i, 0, False)
                if gather_odd:
                    gather(i + 1, 1, False)
                scatter(A, acc1, s_sc1, i, 1, False)

            step_a(0, False)
            with pool.Fori(1, PRE - 1) as i:
                step_a(i, False)
            with pool.Fori(PRE - 1, IT - 1) as i:
                step_a(i, True)
            gather(IT, 0, True)
            scatter(A, acc1, s_sc1, IT - 1, 0, False)
            scatter(A, acc1, s_sc1, IT - 1, 1, False)
            scatter(A, acc1, s_sc1, IT, 0, True)
            pool.wait_ge(s_zero2, 16 * RF)
            rounds(pool, lambda i, par, tail: scatter(B, acc2, s_sc2, i, par, tail))
            scatter(B, acc2, s_sc2, IT, 0, True)

        @block.scalar
        def _(act):
            act.wait_ge(s_set, 1)
            nc.scalar.activation(warm[:, :], eps[:, :], ACT.Sqrt)

            def root(ph, after):
                if after:
                    i, par = after[:2]
                    act.wait_ge(*this(ph["mv_ready"], par, i))
                    nc.scalar.activation(sd[:, par, :], mv[:, par, :, 1], ACT.Sqrt, bias=eps[:, :])\
                        .then_inc(ph["sd_ready"][par], 1)

            def normalise(ph, t, to, i, par, tail, chunks):
                for c, p in chunk_parts(tail)[:chunks]:
                    k = ROWS + c
                    ins = nc.scalar.activation(to[0:p, c, :], t[0:p, c, :], ACT.Identity,
                                               bias=nm[0:p, par, k:k + 1], scale=rs[0:p, par, k:k + 1])
                ins.then_inc(ph["act_normed"][par], 1)

            def relu(ph, i, par, tail):
                act.wait_ge(*this(ph["transposed"], par, i))
                act.wait_ge(*two_ago(ph["product"], par, i))
                for c, p in pieces(tail):
                    ins = nc.scalar.activation(hT[:, par, c, 0:p], psR[:, c, 0:p], ACT.Relu)
                ins.then_inc(ph["relu"][par], 1)

            def copy_sums(ph, i, par, tail):
                p = edge_parts(tail)
                act.wait_ge(*this(ph["summed"], par, i))
                act.wait_ge(*last(ph["v_ready"], par, i))
                nc.scalar.activation(sumT[:, :, 0:p], psA[:, :, 0:p], ACT.Copy)\
                    .then_inc(ph["sum_copied"][par], 1)

            def copy_v(ph, s_sc, i, par, tail):
                p = edge_parts(tail)
                act.wait_ge(*this(ph["v_ready"], par, i))
                act.wait_ge(*two_ago(s_sc, par, i, 64))
                nc.scalar.activation(vrow[0:p, par, :, :], psV[0:p, :, :], ACT.Copy).then_inc(ph["v_copied"][par], 1)

            def body_a(before, now, after):
                i, par, tail, late = now
                p = edge_parts(tail)
                edges = edge_rows(i, par, late)
                act.wait_ge(*this(A["nm_ready"], par, i))
                act.wait_ge(*two_ago(A["summed"], par, i))
                for j in range(ROWS):
                    ins = nc.scalar.activation(hE[0:p, par, j, :], edges[0:p, j, :], ACT.Relu,
                                               bias=nm[0:p, par, j:j + 1], scale=rs[0:p, par, j:j + 1])
                ins.then_inc(A["h_ready"][par], 1)
                act.wait_ge(*two_ago(A["transposed"], par, i))
                normalise(A, rows_a(i, par, tail, late), aux[:, par, :, :], i, par, tail, ACT_A)
                copy_sums(A, i, par, tail)
                relu(A, i, par, tail)
                root(A, after)
                copy_v(A, s_sc1, i, par, tail)

            def histogram(i, par, tail):
                p = edge_parts(tail)
                act.wait_ge(*two_ago(H["used"], par, i))
                act.wait_ge(*this(H["columns"], par, i))
                for j in range(ACT_H):
                    ins = nc.scalar.activation(hotp[0:p, par, j, :], iota_p[0:p, :], ACT.Square,
                                               bias=cols[0:p, par, 2, j:j + 1], scale=-1.0)
                ins.then_inc(H["squared"][par], 1)
                act.wait_ge(*this(H["squared"], par, i))
                nc.scalar.activation(hotp[0:p, par, 0:ACT_H, :], hotp[0:p, par, 0:ACT_H, :], ACT.Relu,
                                     bias=order[0:p, 0, 0:1], scale=-1.0).then_inc(H["ready_p"][par], 1)

            act.wait_ge(s_const, 5)
            act.wait_ge(s_z0, 2)
            rounds(act, histogram)
            histogram(IT, 0, True)

            root(A, (0, 0))
            sweep(act, body_a, (SPILLED, PRE))

            def copy_z(i, par, tail, spill):
                act.wait_ge(*this(B["product"], par, i))
                for c, p in pieces(tail):
                    z = hT[:, par, c, 0:p] if spill else kept(i, par)[:, c, 0:p]
                    ins = nc.scalar.activation(z, psQ[:, c, 0:p], ACT.Copy)
                ins.then_inc(B["z_copied"][par], 1)
                if spill:
                    act.wait_ge(*this(B["z_copied"], par, i))
                    for d, t in spilled(z_dram[2 * (i - KEPT) + par], hT[:, par, :, :], tail):
                        act.dma_start(d, t).then_inc(B["z_stored"][par], 16)

            def body_b(before, now, after, ahead):
                i, par, tail, spill = now
                act.wait_ge(*this(B["nm_ready"], par, i))
                act.wait_ge(*last(B["transposed"], par, i))
                normalise(B, res[:, par, :, :], normed_b, i, par, tail, CHUNKS)
                if before:
                    copy_z(*before)
                if ahead:
                    copy_sums(B, *ahead[:3])
                if spill:
                    act.wait_ge(B["z_stored"][par], (i - KEPT) * 16)
                relu(B, i, par, tail)
                root(B, after)
                if ahead:
                    copy_v(B, s_sc2, *ahead[:3])

            act.wait_ge(s_w, 16 * 13)
            copy_sums(B, 0, 0, False)
            act.wait_ge(*this(s_sc1, 0, IT, 64))
            act.wait_ge(*this(s_sc1, 1, IT - 1, 64))
            copy_v(B, s_sc2, 0, 0, False)
            copy_sums(B, 0, 1, False)
            copy_v(B, s_sc2, 0, 1, False)
            root(B, (0, 0))
            sweep(act, body_b, (KEPT,), wide=True)
            copy_z(IT, 0, True, 1)

            def silu_c(n, i, half, odd, par, tail, fetched):
                act.wait_ge(*this(C["added"], par, n))
                act.wait_ge(*this(C["transposed"], par, n))
                c, p = split_c(tail)[1]
                nc.scalar.activation(z_third(i, par)[:, c, 0:p], ps4[odd][par][:, c, 0:p], ACT.Silu,
                                     bias=vecs[:, 0:1])
                for c, p in split_c(tail)[0]:
                    t = z_third(i, par)[:, c, 0:p]
                    ins = nc.scalar.activation(t, t, ACT.Silu, bias=vecs[:, 0:1])
                ins.then_inc(C["silu"][par], 1)

            nc.scalar.activation(warm[:, :], eps[:, :], ACT.Silu)
            walk_c(act, silu_c)

            def bn_root(k):
                act.wait_ge(s_bn[k], 1)
                nc.scalar.activation(bn[:, k, 2:3], bn[:, k, 1:2], ACT.Sqrt, bias=eps[:, :]).then_inc(s_bn[k], 1)

            bn_root(0)
            act.wait_ge(s_bn[0], 8)
            nc.scalar.activation(warm[:, :], eps[:, :], ACT.Silu)

            def silu_f(n, i, par, tail):
                act.wait_ge(*this(F["product"], par, n))
                for c, p in pieces(tail):
                    ins = nc.scalar.activation(z_later(i, par)[:, c, 0:p], ps2[par][:, c, 0:p], ACT.Silu,
                                               bias=bn[:, 0, 7:8])
                ins.then_inc(F["silu"][par], 1)

            walk_f(act, silu_f)
            bn_root(1)
            act.wait_ge(s_bn[1], 6)
            for par in range(2):
                act.wait_ge(F["stored"][par], 48)

            def scale_g(i, par, tail):
                is_late = type(i) is int and i >= KEPT_LATER
                if is_late:
                    act.wait_ge(*late(i, par, tail, 3))
                act.wait_ge(*two_ago(G["product"], par, i))
                z = kept(i - KEPT_LATER if is_late else i, par)
                for c, p in pieces(tail):
                    ins = nc.scalar.activation(hT[:, par, c, 0:p], z[:, c, 0:p], ACT.Identity,
                                               bias=bn[:, 1, 6:7], scale=bn[:, 1, 4:5])
                ins.then_inc(G["scaled"][par], 1)

            rounds(act, scale_g, 0, KEPT_LATER)
            for r in late_rounds():
                scale_g(*r)

        @block.vector
        def _(dve):
            done = [0]

            def link(ins):
                done[0] += 1
                ins.then_inc(s_chain, 1)
                dve.wait_ge(s_chain, done[0])

            nc.vector.memset(eps[:, :], EPS).then_inc(s_set, 1)
            nc.vector.memset(zeros[:, :], 0.0).then_inc(s_set, 1)
            nc.vector.memset(hots, 0.0).then_inc(s_z0, 1)
            link(nc.vector.memset(mv[:, :, :, :], 1.0))
            dve.wait_ge(s_z0, 2)
            dve.wait_ge(s_idx, 64)
            dve.wait_ge(s_const, 5)
            for k, tab in enumerate((dst_tab, src_tab)):
                r3 = raw[:, k, :].rearrange("p (r j) -> p r j", j=ROWS)
                link(nc.vector.tensor_copy(tab[:, :, 0, :], r3))
                for j in range(ROWS):
                    ins = nc.vector.tensor_scalar(tab[:, :, 1, j], tab[:, :, 0, j], -1.0, dump[:, j:j + 1],
                                                  ALU.mult, ALU.add)
                link(ins)
            link(nc.vector.tensor_scalar(ints[:, 0, :], raw[:, 0, :], 2, P - 1, ALU.logical_shift_right,
                                         ALU.bitwise_and))
            nc.vector.tensor_copy(dst_tab[:, :, 2, :], ints[:, 0, :].rearrange("p (r j) -> p r j", j=ROWS))
            link(nc.vector.tensor_scalar(ints[:, 1, :], raw[:, 0, :], 9, None, ALU.logical_shift_right))
            link(nc.vector.tensor_scalar(ints[:, 0, :], raw[:, 0, :], ROWS - 1, None, ALU.bitwise_and))
            link(nc.vector.scalar_tensor_tensor(
                dst_tab[:, :, 3, :], ints[:, 1, :].rearrange("p (r j) -> p r j", j=ROWS), float(ROWS),
                ints[:, 0, :].rearrange("p (r j) -> p r j", j=ROWS), ALU.mult, ALU.add))

            chain = {"at": 0, "n": 0}

            def signal(ins):
                chain["n"] += 1
                ins.then_inc(s_chain, 1)

            def settle():
                dve.wait_ge(s_chain, chain["at"] + chain["n"])

            def link_(ins):
                signal(ins)
                settle()

            def aim(ph, i, par, tail, *_):
                p = edge_parts(tail)
                dve.wait_ge(*two_ago(s_sc1 if ph is A else s_sc2, par, i, 64))
                nc.vector.tensor_tensor(target[0:p, par, :], shift[0:p, par, :], cols[0:p, par, 0, :], ALU.add)\
                    .then_inc(ph["targets"][par], 1)

            def compare(ph, i, par, tail):
                p = edge_parts(tail)
                dve.wait_ge(*this(ph["row_loaded"], par, i, 16))
                dve.wait_ge(*two_ago(ph["summed"], par, i))
                row = irow[0:p, par, 0:p * ROWS].rearrange("p (q j) -> p j q", j=ROWS)
                for j in range(ROWS):
                    at = j * (j + 1) // 2
                    ins = nc.vector.scalar_tensor_tensor(
                        same[0:p, par, at:at + j + 1, 0:p], row[:, 0:j + 1, :], cols[0:p, par, 0, j:j + 1],
                        order[0:p, ROWS - 1 - j:ROWS, 0:p], ALU.is_equal, ALU.mult,
                        accum_out=count[0:p, par, j:j + 1])
                link_(ins)
                nc.vector.scalar_tensor_tensor(shift[0:p, par, :], count[0:p, par, :], 1.5, cols[0:p, par, 1, :],
                                               ALU.is_gt, ALU.mult).then_inc(ph["compared"][par], 1)

            def scales(ph, i, par):
                dve.wait_ge(*this(ph["sd_ready"], par, i))
                dve.wait_ge(*two_ago(ph["act_normed"], par, i))
                if ph is A:
                    dve.wait_ge(*two_ago(A["h_ready"], par, i))
                link_(nc.vector.reciprocal(rs[:, par, :], sd[:, par, :]))
                nc.vector.scalar_tensor_tensor(nm[:, par, :], mv[:, par, :, 0], -1.0, rs[:, par, :],
                                               ALU.mult, ALU.mult).then_inc(ph["nm_ready"][par], 1)

            def chained(body, per):
                def run(before, now, *others):
                    chain["at"] = done[0] + (2 * now[0] + now[1]) * per
                    chain["n"] = 0
                    body(before, now, *others)
                    assert chain["n"] == per, chain["n"]
                return run

            def histogram(i, par, tail):
                p = edge_parts(tail)
                dve.wait_ge(*two_ago(H["used"], par, i))
                nc.vector.tensor_copy(cols[:, par, :, :], dst_tab[:, 2 * i + par, :, :]).then_inc(H["columns"][par], 1)
                dve.wait_ge(*this(H["columns"], par, i))
                for j in range(ACT_H, ROWS):
                    nc.vector.tensor_scalar(hotp[0:p, par, j, :], iota_p[0:p, :], cols[0:p, par, 2, j:j + 1], None,
                                            ALU.is_equal)
                for j in range(ROWS):
                    ins = nc.vector.tensor_scalar(hotc[0:p, par, j, :], iota_c[0:p, :], cols[0:p, par, 3, j:j + 1],
                                                  None, ALU.is_equal)
                ins.then_inc(H["ready_c"][par], 1)

            rounds(dve, histogram)
            histogram(IT, 0, True)
            dve.wait_ge(*this(H["used"], 0, IT))

            def add_a(i, par, tail, late):
                dve.wait_ge(*this(A["product"], par, i))
                x_t = rows_a(i, par, tail, late)
                y_t = res[:, par, :, :] if tail else x_t
                for c, q in pieces(tail):
                    ins = nc.vector.tensor_tensor(y_t[0:q, c, :], psQ[0:q, c, :], x_t[0:q, c, :], ALU.add)
                ins.then_inc(A["added"][par], 1)

            def body_a(before, now, after):
                i, par, tail, late = now
                p = edge_parts(tail)
                dve.wait_ge(*((A["x_loaded"][0], 16 * (IT + 2)) if tail else this(A["x_loaded"], par, i, 16)))
                x_t = rows_a(i, par, tail, late)
                for c, q in chunk_parts(tail):
                    nc.vector.bn_stats(st6[0:q, par, ROWS + c, :], x_t[0:q, c, :])
                if gathered(i, par, late):
                    dve.wait_ge(*gathers(A["rows_loaded"], par, i + 1, 64))
                else:
                    dve.wait_ge(s_pre, 64 * PRE)
                for j in range(ROWS):
                    ins = nc.vector.bn_stats(st6[0:p, par, j, :], edge_rows(i, par, late)[0:p, j, :])
                signal(ins)
                if two_back(*now):
                    add_a(*two_back(*now))
                if before:
                    aim(A, *before)
                settle()
                nc.vector.tensor_copy(cols[:, par, :, :], dst_tab[:, round_a_of(i, par, tail, late), :, :])
                for c, q in chunk_parts(tail):
                    nc.vector.bn_aggr(mv[0:q, par, ROWS + c, :], st6[0:q, par, ROWS + c, :])
                for j in range(ROWS):
                    ins = nc.vector.bn_aggr(mv[0:p, par, j, :], st6[0:p, par, j, :])
                ins.then_inc(A["mv_ready"][par], 1)
                dve.wait_ge(*this(A["mv_ready"], par, i))
                compare(A, i, par, tail)
                scales(A, i, par)
                dve.wait_ge(*two_ago(A["transposed"], par, i))
                for c, q in chunk_parts(tail)[ACT_A:]:
                    k = ROWS + c
                    ins = nc.vector.tensor_scalar(aux[0:q, par, c, :], x_t[0:q, c, :], mv[0:q, par, k, 0:1],
                                                  rs[0:q, par, k:k + 1], ALU.subtract, ALU.mult)
                ins.then_inc(A["normed"][par], 1)

            sweep(dve, chained(body_a, 3), (SPILLED, PRE))
            done[0] += (RF + 1) * 3
            add_a(IT - 1, 1, False, 2)
            aim(A, IT, 0, True)
            link(nc.vector.tensor_scalar(rdeg[:, :], psH, 1.0, None, ALU.max))
            link(nc.vector.reciprocal(rdeg[:, :], rdeg[:, :]))
            chain["at"], chain["n"] = done[0], 0
            dve.wait_ge(*this(A["summed"], 0, IT))
            dve.wait_ge(*this(A["summed"], 1, IT - 1))
            for par in range(2):
                link_(nc.vector.tensor_copy(cols[:, par, 0:2, :], src_tab[:, par, :, :]))
                compare(B, 0, par, False)
                dve.wait_ge(*this(B["compared"], par, 0))
            done[0] += chain["n"]
            add_a(IT, 0, True, 2)
            dve.wait_ge(*this(s_sc1, 0, IT, 64))
            dve.wait_ge(*this(s_sc1, 1, IT - 1, 64))
            aim(B, 0, 0, False)
            def body_b(before, now, after, ahead):
                i, par, tail, spill = now
                r = 2 * i + par
                if spill:
                    dve.wait_ge(B["y_loaded"][par], (i - KEPT + 1) * 16 + (16 if tail else 0))
                dve.wait_ge(*((B["a_loaded"][0], 16 * (IT + 2)) if tail else this(B["a_loaded"], par, i, 16)))
                dve.wait_ge(*two_ago(B["stored"], par, i, 16))
                dve.wait_ge(*two_ago(B["act_normed"], par, i))
                y = xin[:, par, :, :] if spill else kept(i, par)
                for c, q in chunk_parts(tail):
                    deg = rdeg[0:q, bass.ds(r * CHUNKS + c, 1)]
                    ins = nc.vector.scalar_tensor_tensor(res[0:q, par, c, :], aux[0:q, par, c, :], deg, y[0:q, c, :],
                                                         ALU.mult, ALU.add)
                ins.then_inc(B["added"][par], 1)
                dve.wait_ge(*this(B["added"], par, i))
                for c, q in chunk_parts(tail):
                    ins = nc.vector.bn_stats(st6[0:q, par, ROWS + c, :], res[0:q, par, c, :])
                signal(ins)
                if after:
                    aim(B, *after)
                settle()
                if ahead:
                    nc.vector.tensor_copy(cols[:, par, 0:2, :], src_tab[:, r + 2, :, :])
                for c, q in chunk_parts(tail):
                    ins = nc.vector.bn_aggr(mv[0:q, par, ROWS + c, :], st6[0:q, par, ROWS + c, :])
                ins.then_inc(B["mv_ready"][par], 1)
                if ahead:
                    dve.wait_ge(*this(B["mv_ready"], par, i))
                    compare(B, *ahead[:3])
                else:
                    dve.sem_inc(s_chain, 1)
                    chain["n"] += 1
                scales(B, i, par)

            sweep(dve, chained(body_b, 3), (KEPT,), wide=True)
            done[0] += (RF + 1) * 3

            def count_batch(ph, n, i, par, tail, place=z_later):
                dve.wait_ge(*this(ph["silu"], par, n))
                for half in range(2):
                    p = NODE_TAIL[half] if tail else P
                    c = slice(half * ROWS, (half + 1) * ROWS)
                    ins = nc.vector.bn_stats(bst[:, bass.ds((2 * i + par) * 2 + half, 1), :]
                                             .rearrange("p a s -> p (a s)"), place(i, par)[:, c, 0:p])
                ins.then_inc(ph["stats"][par], 1)

            def add_c(n, i, half, odd, par, tail, fetched):
                dve.wait_ge(*this(C["transposed"], par, n))
                if returned(i, par, tail, fetched):
                    dve.wait_ge(*returned(i, par, tail, fetched))
                for c, p in split_c(tail)[0]:
                    t = z_third(i, par)[:, c, 0:p]
                    ins = nc.vector.tensor_tensor(t, ps4[odd][par][:, c, 0:p], t, ALU.add)
                ins.then_inc(C["added"][par], 1)
                if par:
                    count_batch(C, n, i, 0, False)
                elif type(n) is not int:
                    count_batch(C, n - 1, i - 1, 1, False)
                elif n > 0:
                    count_batch(C, n - 1, iteration_c(n - 1), 1, False)

            walk_c(dve, add_c)
            count_batch(C, IT, IT, 0, True, place=z_third)

            def fold(k, sems):
                dve.wait_ge(*this(sems, 1, IT - 1))
                dve.wait_ge(*this(sems, 0, IT))
                nc.vector.bn_aggr(bn[:, k, 0:2], bst[:, :, :].rearrange("p a s -> p (a s)")).then_inc(s_bn[k], 1)
                dve.wait_ge(s_bn[k], 2)
                nc.vector.reciprocal(bn[:, k, 3:4], bn[:, k, 2:3]).then_inc(s_bn[k], 1)
                dve.wait_ge(s_bn[k], 3)
                nc.vector.tensor_tensor(bn[:, k, 4:5], bn[:, k, 3:4], vecs[:, 3 * k + 1:3 * k + 2], ALU.mult)\
                    .then_inc(s_bn[k], 1)
                dve.wait_ge(s_bn[k], 4)
                nc.vector.tensor_tensor(bn[:, k, 5:6], bn[:, k, 4:5], bn[:, k, 0:1], ALU.mult).then_inc(s_bn[k], 1)
                dve.wait_ge(s_bn[k], 5)
                nc.vector.tensor_tensor(bn[:, k, 6:7], vecs[:, 3 * k + 2:3 * k + 3], bn[:, k, 5:6], ALU.subtract)\
                    .then_inc(s_bn[k], 1)

            dve.wait_ge(s_w, 16 * 13)
            fold(0, C["stats"])
            nc.vector.tensor_scalar(w2s[:, :], w2[:, :], bn[:, 0, 4:5], None, ALU.mult).then_inc(s_bn[0], 1)
            dve.wait_ge(s_bw, 1)
            nc.vector.tensor_tensor(bn[:, 0, 7:8], psB[:, 0:1], vecs[:, 3:4], ALU.add).then_inc(s_bn[0], 1)

            walk_f(dve, lambda *step: count_batch(F, *step))
            fold(1, F["stats"])

            def finish(i, half, odd, par, tail=False):
                dve.wait_ge(x1_loaded[odd][par], 16 * (half + (2 if tail else 1)))
                chain["at"], chain["n"] = done[0] + 2 * i + par, 0
                t = x1_place(i, par)
                for c, q in pieces(tail):
                    b3c = b3b[0:q, :].unsqueeze(1).broadcast_to([q, c.stop - c.start, D])
                    ins = nc.vector.tensor_tensor(t[0:q, c, :], t[0:q, c, :], b3c, ALU.add)
                link_(ins)
                dve.wait_ge(*this(G["product"], par, i))
                for c, q in pieces(tail):
                    ins = nc.vector.tensor_tensor(t[0:q, c, :], t[0:q, c, :], ps2[par][0:q, c, :], ALU.add)
                ins.then_inc(G["done"][par], 1)

            for i in range(3):
                for par in range(2):
                    finish(i, i // 2, i % 2, par)
            doubled(dve, finish, 3, IT - 1)
            for i, par, tail in late_rounds()[4:]:
                finish(i, i // 2, i % 2, par, tail)

        @block.tensor
        def _(pe):
            pe.wait_ge(s_const, 5)
            pe.wait_ge(s_w, 16 * 13)
            pe.wait_ge(s_z0, 1)
            nc.tensor.matmul(psH, hotp[:, 0, 0, :], hotc[:, 0, 0, :], start=True, stop=False).then_inc(s_z0, 1)

            def count_edges(i, par, tail):
                p = edge_parts(tail)
                pe.wait_ge(*this(H["ready_p"], par, i))
                pe.wait_ge(*this(H["ready_c"], par, i))
                for j in range(ROWS):
                    ins = nc.tensor.matmul(psH, hotp[0:p, par, j, :], hotc[0:p, par, j, :], start=False,
                                           stop=bool(tail and j == ROWS - 1))
                ins.then_inc(H["used"][par], 1)

            rounds(pe, count_edges)
            count_edges(IT, 0, True)

            def transposes(t, ps_t, tail):
                for c, p in chunk_parts(tail):
                    ins = nc.tensor.transpose(ps_t[:, c, 0:p], t[0:p, c, :], ident[0:p, 0:p])
                return ins

            def presum(t, par, tail):
                p = edge_parts(tail)
                for j in reversed(range(ROWS)):
                    at = j * (j + 1) // 2
                    ins = nc.tensor.matmul(psA[:, 0:j + 1, 0:p], t[0:p, j, :], same[0:p, par, at:at + j + 1, 0:p],
                                           start=(j == ROWS - 1), stop=(j == 0))
                return ins

            def edge_product(w, par, tail):
                p = edge_parts(tail)
                for j in range(ROWS):
                    ins = nc.tensor.matmul(psV[0:p, j, :], sumT[:, j, 0:p], w[:, :], start=True, stop=True)
                return ins

            def round_a(i, par, tail):
                pe.wait_ge(*this(A["h_ready"], par, i))
                pe.wait_ge(*this(A["compared"], par, i))
                pe.wait_ge(*last(A["sum_copied"], par, i))
                presum(hE[:, par, :, :], par, tail).then_inc(A["summed"][par], 1)
                pe.wait_ge(*this(A["normed"], par, i))
                pe.wait_ge(*this(A["act_normed"], par, i))
                pe.wait_ge(*last(A["relu"], par, i))
                transposes(aux[:, par, :, :], psR, tail).then_inc(A["transposed"][par], 1)
                pe.wait_ge(*this(A["sum_copied"], par, i))
                pe.wait_ge(*last(A["v_copied"], par, i))
                edge_product(wl, par, tail).then_inc(A["v_ready"][par], 1)
                pe.wait_ge(*this(A["relu"], par, i))
                pe.wait_ge(*last(A["added"], par, i))
                for c, q in chunk_parts(tail):
                    ins = nc.tensor.matmul(psQ[0:q, c, :], hT[:, par, c, 0:q], wr[:, :], start=True, stop=True)
                ins.then_inc(A["product"][par], 1)

            rounds(pe, round_a)
            round_a(IT, 0, True)

            def sum_edges_b(i, par, tail, *_):
                pe.wait_ge(*this(B["rows_loaded"], par, i, 16))
                pe.wait_ge(*this(B["compared"], par, i))
                pe.wait_ge(*last(B["sum_copied"], par, i))
                presum(rows[:, par, :, :], par, tail).then_inc(B["summed"][par], 1)

            def multiply_edges_b(i, par, tail, *_):
                pe.wait_ge(*this(B["sum_copied"], par, i))
                pe.wait_ge(*last(B["v_copied"], par, i))
                edge_product(w1b, par, tail).then_inc(B["v_ready"][par], 1)

            def round_b(before, now, after, ahead):
                i, par, tail, spill = now
                if ahead:
                    sum_edges_b(*ahead)
                pe.wait_ge(*this(B["act_normed"], par, i))
                pe.wait_ge(*last(B["relu"], par, i))
                transposes(normed_b, psR, tail).then_inc(B["transposed"][par], 1)
                if ahead:
                    multiply_edges_b(*ahead)
                pe.wait_ge(*this(B["relu"], par, i))
                pe.wait_ge(*last(B["z_copied"], par, i))
                for n in range(2):
                    q = NODE_TAIL[n] if tail else P
                    c = slice(n * ROWS, (n + 1) * ROWS)
                    ins = nc.tensor.matmul(psQ[:, c, 0:q], w1a[:, :], hT[:, par, c, 0:q], start=True, stop=True)
                ins.then_inc(B["product"][par], 1)

            for par in range(2):
                sum_edges_b(0, par, False)
                multiply_edges_b(0, par, False)
            sweep(pe, round_b, (KEPT,), wide=True)

            def round_c(n, i, half, odd, par, tail, fetched):
                if not tail:
                    pe.wait_ge(acc2_loaded[odd][par], 16 * (half + 1))
                if type(n) is not int or n >= 2:
                    pe.wait_ge(C["added"][par], n - 1)
                    pe.wait_ge(C["silu"][par], n - 1)
                if returned(i, par, tail, fetched):
                    pe.wait_ge(*returned(i, par, tail, fetched))
                rows_c = acc2_place(n, odd, par)
                c, p = split_c(tail)[1]
                nc.tensor.matmul(ps4[odd][par][:, c, 0:p], ident[:, :], z_third(i, par)[:, c, 0:p],
                                 start=True, stop=False)
                for k in range(DVE_C, CHUNKS):
                    nc.tensor.matmul(ps4[odd][par][:, k, 0:p], rows_c[0:p, k, :], ident[0:p, 0:p], start=False,
                                     stop=(k == CHUNKS - 1))
                for k, q in chunk_parts(tail)[:DVE_C]:
                    ins = nc.tensor.transpose(ps4[odd][par][:, k, 0:q], rows_c[0:q, k, :], ident[0:q, 0:q])
                ins.then_inc(C["transposed"][par], 1)

            pe.wait_ge(*this(B["relu"], 0, IT))
            pe.wait_ge(*this(B["z_copied"], 0, IT))
            walk_c(pe, round_c)

            pe.wait_ge(s_bn[0], 7)
            nc.tensor.matmul(psB[:, 0:1], w2[:, :], bn[:, 0, 6:7], start=True, stop=True).then_inc(s_bw, 1)

            def round_f(n, i, par, tail):
                pe.wait_ge(*two_ago(F["silu"], par, n))
                if type(i) is int and i >= KEPT_LATER:
                    pe.wait_ge(*late(i, par, tail, 2))
                for n in range(2):
                    q = NODE_TAIL[n] if tail else P
                    c = slice(n * ROWS, (n + 1) * ROWS)
                    ins = nc.tensor.matmul(ps2[par][:, c, 0:q], w2s[:, :], z_later(i, par)[:, c, 0:q],
                                           start=True, stop=True)
                ins.then_inc(F["product"][par], 1)

            walk_f(pe, round_f)

            def round_g(i, par, tail):
                pe.wait_ge(*this(G["scaled"], par, i))
                pe.wait_ge(*two_ago(G["done"], par, i))
                for c, q in chunk_parts(tail):
                    ins = nc.tensor.matmul(ps2[par][0:q, c, :], hT[:, par, c, 0:q], w3[:, :], start=True, stop=True)
                ins.then_inc(G["product"][par], 1)

            pe.wait_ge(*this(F["silu"], 0, IT))
            pe.wait_ge(*this(F["silu"], 1, IT - 1))
            rounds(pe, round_g)
            round_g(IT, 0, True)


_ARGS = ["x", "src", "dst", "edge_attr_128", "L0_gnn_W_l", "L0_gnn_W_r", "L1_gnn_W1", "L1_gnn_b1", "L1_gnn_g1",
         "L1_gnn_be1", "L1_gnn_W2", "L1_gnn_b2", "L1_gnn_g2", "L1_gnn_be2", "L1_gnn_W3", "L1_gnn_b3"]


def kernel(**inputs):
    import numpy as _np
    import concourse.bacc as _bacc
    from concourse import mybir as _mybir
    from concourse.bass_utils import run_bass_kernel_spmd as _run

    nc = _bacc.Bacc("TRN2", target_bir_lowering=False, num_devices=1)
    arrays, args = {}, []
    for name in _ARGS:
        a = _np.asarray(inputs[name])
        if name in ("L0_gnn_W_l", "L0_gnn_W_r"):
            a = a.T
        a = _np.ascontiguousarray(a)
        arrays[f"in_{name}_dram"] = a
        args.append(nc.dram_tensor(f"in_{name}_dram", a.shape, _mybir.dt.from_np(a.dtype), kind="ExternalInput").ap())
    shape = tuple(inputs["x"].shape)
    args.append(nc.dram_tensor("out_0_dram", shape, _mybir.dt.float32, kind="ExternalOutput").ap())
    gnn_layers(nc, *args)
    r = _run(nc, [arrays], core_ids=[0])
    return r.results[0]["out_0_dram"]
```
